# Optimizing a Trainium2 kernel written in Bass

```python
import numpy as np
import jax
import jax.numpy as jnp

def _softmax(x, axis=-1):
    return jax.nn.softmax(x, axis=axis)

def _gelu(x):
    return jax.nn.gelu(x, approximate=True)

def _silu(x):
    return jax.nn.silu(x)

def _sigmoid(x):
    return jax.nn.sigmoid(x)

def _layernorm(x, axis=-1, eps=1e-05):
    m = jnp.mean(x, axis=axis, keepdims=True)
    v = jnp.var(x, axis=axis, keepdims=True)
    return (x - m) / jnp.sqrt(v + eps)

def _scatter_add(tgt, idx, src, axis=0):
    return tgt.at[idx].add(src)

def _segment_sum(src, seg, n):
    return jax.ops.segment_sum(src, seg, n)
kernel_name = 'mk_prb_d1_jaxref_r8_6c5516'

def setup_inputs(seed: int=0):
    np.random.seed(seed)
    _w = jnp.asarray

    def _L0_attn_setup():
        import jax, jax.numpy as jnp
        import numpy as np
        DIM, H, G = (128, 16, 4)
        HD = DIM // H
        HKV = H // G

        def rotate_half(x):
            return jnp.concatenate([-x[..., 1::2], x[..., ::2]], axis=-1)

        def rope_tables(seq_len, dim, dtype):
            inv_freq = 1.0 / 10000.0 ** (jnp.arange(0, dim, 2, dtype=jnp.float32) / dim)
            pos = jnp.arange(seq_len, dtype=jnp.float32)
            sinusoid = pos[:, None] * inv_freq[None, :]
            sin = jnp.concatenate([jnp.sin(sinusoid)] * 2, -1)
            cos = jnp.concatenate([jnp.cos(sinusoid)] * 2, -1)
            return (sin.astype(dtype)[None, :, None, :], cos.astype(dtype)[None, :, None, :])
        key = jax.random.key(seed)
        ks = jax.random.split(key, 9)
        s = 0.02
        return {'hidden_states': jax.random.normal(ks[0], (2, 256, DIM), jnp.float32), 'Wq': jax.random.normal(ks[1], (DIM, DIM), jnp.float32) * s, 'bq': jnp.zeros((DIM,), jnp.float32), 'Wk': jax.random.normal(ks[2], (DIM // G, DIM), jnp.float32) * s, 'bk': jnp.zeros((DIM // G,), jnp.float32), 'Wv': jax.random.normal(ks[3], (DIM // G, DIM), jnp.float32) * s, 'bv': jnp.zeros((DIM // G,), jnp.float32), 'Wo': jax.random.normal(ks[4], (DIM, DIM), jnp.float32) * s, 'bo': jnp.zeros((DIM,), jnp.float32)}
    _L0_attn_in = _L0_attn_setup()

    def _L0_ffn_setup():
        import jax, jax.numpy as jnp
        import numpy as np
        DIM = 128
        HIDDEN = 384
        SCALE = 1.0 / 127.0

        def _dequant(w_int, dtype):
            return w_int.astype(dtype) * jnp.asarray(SCALE, dtype)
        key = jax.random.key(seed)
        k_x, k_g, k_u, k_d = jax.random.split(key, 4)
        x = jax.random.normal(k_x, (4, 256, DIM), dtype=jnp.float32)
        w_gate = jax.random.randint(k_g, (HIDDEN, DIM), -127, 128, dtype=jnp.int32)
        w_up = jax.random.randint(k_u, (HIDDEN, DIM), -127, 128, dtype=jnp.int32)
        w_down = jax.random.randint(k_d, (DIM, HIDDEN), -127, 128, dtype=jnp.int32)
        return {'x': x, 'w_gate': w_gate, 'w_up': w_up, 'w_down': w_down}
    _L0_ffn_in = _L0_ffn_setup()
    _d = {'L0_attn_hidden_states': _L0_attn_in['hidden_states'], 'L0_attn_Wq': _L0_attn_in['Wq'], 'L0_attn_bq': _L0_attn_in['bq'], 'L0_attn_Wk': _L0_attn_in['Wk'], 'L0_attn_bk': _L0_attn_in['bk'], 'L0_attn_Wv': _L0_attn_in['Wv'], 'L0_attn_bv': _L0_attn_in['bv'], 'L0_attn_Wo': _L0_attn_in['Wo'], 'L0_attn_bo': _L0_attn_in['bo'], 'L0_ffn_w_gate': _L0_ffn_in['w_gate'], 'L0_ffn_w_up': _L0_ffn_in['w_up'], 'L0_ffn_w_down': _L0_ffn_in['w_down']}
    _x0 = _d['L0_attn_hidden_states']
    _d['L0_attn_hidden_states'] = jax.random.normal(jax.random.fold_in(jax.random.key(seed), 1), (4, 1024, 128), dtype=_x0.dtype)
    del _x0
    return _d

def reference(L0_attn_hidden_states, L0_attn_Wq, L0_attn_bq, L0_attn_Wk, L0_attn_bk, L0_attn_Wv, L0_attn_bv, L0_attn_Wo, L0_attn_bo, L0_ffn_w_gate, L0_ffn_w_up, L0_ffn_w_down):

    def _L0_attn_ref(hidden_states, Wq, bq, Wk, bk, Wv, bv, Wo, bo):
        import jax, jax.numpy as jnp
        import numpy as np
        DIM, H, G = (128, 16, 4)
        HD = DIM // H
        HKV = H // G

        def rotate_half(x):
            return jnp.concatenate([-x[..., 1::2], x[..., ::2]], axis=-1)

        def rope_tables(seq_len, dim, dtype):
            inv_freq = 1.0 / 10000.0 ** (jnp.arange(0, dim, 2, dtype=jnp.float32) / dim)
            pos = jnp.arange(seq_len, dtype=jnp.float32)
            sinusoid = pos[:, None] * inv_freq[None, :]
            sin = jnp.concatenate([jnp.sin(sinusoid)] * 2, -1)
            cos = jnp.concatenate([jnp.cos(sinusoid)] * 2, -1)
            return (sin.astype(dtype)[None, :, None, :], cos.astype(dtype)[None, :, None, :])
        b, t, _ = hidden_states.shape
        q = (hidden_states @ Wq.T + bq).reshape(b, t, H, HD)
        k = (hidden_states @ Wk.T + bk).reshape(b, t, HKV, HD)
        v = (hidden_states @ Wv.T + bv).reshape(b, t, HKV, HD)
        sin, cos = rope_tables(t, HD, q.dtype)
        q = q * cos + rotate_half(q) * sin
        k = k * cos + rotate_half(k) * sin
        k = jnp.repeat(k, G, axis=2)
        v = jnp.repeat(v, G, axis=2)
        scale = 1.0 / jnp.sqrt(jnp.float32(HD)).astype(q.dtype)
        scores = jnp.einsum('bthd,bshd->btsh', q, k) * scale
        probs = jax.nn.softmax(scores, axis=2)
        context = jnp.einsum('btsh,bshd->bthd', probs, v).reshape(b, t, DIM)
        return context @ Wo.T + bo

    def _L0_ffn_ref(x, w_gate, w_up, w_down):
        import jax, jax.numpy as jnp
        import numpy as np
        DIM = 128
        HIDDEN = 384
        SCALE = 1.0 / 127.0

        def _dequant(w_int, dtype):
            return w_int.astype(dtype) * jnp.asarray(SCALE, dtype)
        wg = _dequant(w_gate, x.dtype)
        wu = _dequant(w_up, x.dtype)
        wd = _dequant(w_down, x.dtype)
        gate = jnp.einsum('bsd,hd->bsh', x, wg)
        up = jnp.einsum('bsd,hd->bsh', x, wu)
        h = jax.nn.silu(gate) * up
        return jnp.einsum('bsh,dh->bsd', h, wd)
    x = L0_attn_hidden_states
    xn = _layernorm(x, axis=-1)
    x = x + _L0_attn_ref(xn, L0_attn_Wq, L0_attn_bq, L0_attn_Wk, L0_attn_bk, L0_attn_Wv, L0_attn_bv, L0_attn_Wo, L0_attn_bo) + _L0_ffn_ref(xn, L0_ffn_w_gate, L0_ffn_w_up, L0_ffn_w_down)
    return x

_drawn_inputs = setup_inputs


def setup_inputs(seed=0):
    import zlib

    import numpy as np

    out = dict(_drawn_inputs(seed))
    spreads = {'L0_attn_bq': (0.0, 2.0),
     'L0_attn_bk': (0.0, 2.0),
     'L0_attn_bv': (0.0, 2.0),
     'L0_attn_bo': (0.0, 2.0)}
    factors = {'L0_attn_Wq': 64.0, 'L0_attn_Wk': 64.0, 'L0_attn_Wv': 64.0, 'L0_attn_Wo': 64.0}
    for name, (base, spread) in spreads.items():
        noise = np.random.default_rng([zlib.crc32(name.encode()), seed]).standard_normal(out[name].shape)
        drawn = base * np.exp(spread * noise) if base else spread * noise
        out[name] = jnp.asarray(drawn.astype(out[name].dtype))
    for name, factor in factors.items():
        out[name] = (out[name] * factor).astype(out[name].dtype)
    return out
```

```python
from contextlib import ExitStack

import concourse.bass as bass
from concourse import mybir

F32 = mybir.dt.float32
BF16 = mybir.dt.bfloat16
I32 = mybir.dt.int32
ALU = mybir.AluOpType
ACT = mybir.ActivationFunctionType
AX = mybir.AxisListType

B, T, D = 4, 1024, 128
H, G = 16, 4
HD = D // H
KV = H // G
HID = 384
P = 128
W = 512
NT = T // P
NTT = B * NT
NG = B * KV
PARTS = 3
ROWS = PARTS * PARTS * HD
MAX_ROW = 96
NQ = T // W
STEPS = NQ * NT
UNITS = 2
SLOTS = 2
AU = G * NT * NQ
RING = 3
LAST_A = 14
A_OF = [AU * (s + 1) // LAST_A - AU * s // LAST_A if s < LAST_A else 0 for s in range(STEPS)]
CH = T * B // NG
CT = CH // P
FC = HID // P
VC = 32
SCALE = HD ** -0.5
DEQUANT = 1.0 / 127.0
EPS = 1e-5
C_Q, C_QR, C_K, C_KR, C_V, C_O = 0, D, 2 * D, 2 * D + 32, 2 * D + 64, 2 * D + 96
C_ALL = C_O + D


def attention_swiglu(nc, x, wf, wi, biases, bo, tables, identity, out):
    q_parts = nc.dram_tensor("q_parts", (NG, PARTS * HD, G, T), BF16, kind="Internal").ap()
    k_parts = nc.dram_tensor("k_parts", (NG, PARTS, HD, T), BF16, kind="Internal").ap()

    with ExitStack() as ctx:
        def sb(name, shape, dt=F32):
            return ctx.enter_context(nc.sbuf_tensor(name, shape, dt))

        def sem(name):
            return ctx.enter_context(nc.semaphore(name))

        ident = sb("ident", [P, P])
        ident16 = sb("ident16", [P, P], BF16)
        wf_sb = sb("wf_sb", [P, C_ALL])
        wi_sb = sb("wi_sb", [P, 3 * HID], I32)
        w_ffn = sb("w_ffn", [P, 3 * HID])
        bias_sb = sb("bias_sb", [P, 5])
        bo_sb = sb("bo_sb", [P, D])
        rope = sb("rope", [P, 2, T])
        y_all = sb("y_all", [P, NTT, D])
        xn_T = sb("xn_T", [P, B * T])
        ctx_all = sb("ctx_all", [P, NG, NT * G * HD])
        v_all = sb("v_all", [P, NT, NG, HD])
        v_grp = [sb(f"v_grp{i}", [P, NT, VC]) for i in range(2)]
        qa = [sb(f"qa{i}", [P, G, T], BF16) for i in range(2)]
        ka = [sb(f"ka{i}", [P, T], BF16) for i in range(2)]
        qc = [sb(f"qc{i}", [P, G, T], BF16) for i in range(2)]
        kc = [sb(f"kc{i}", [P, T], BF16) for i in range(2)]
        probs = sb("probs", [P, SLOTS, G, W])
        acc_sb = sb("acc_sb", [P, NQ, W])
        mx = sb("mx", [P, G * NT, NQ])
        row_max = sb("row_max", [P, G * NT])
        rest = sb("rest", [P, G * NT])
        neg_max = sb("neg_max", [P, PARTS, G * NT], BF16)
        neg_max_T = sb("neg_max_T", [PARTS * G * NT, P], BF16)
        th = sb("th", [P, FC, CH])
        gated = sb("gated", [P, FC, CH])
        hid = sb("hid", [P, FC, CH])
        rec = sb("rec", [P, NQ, NT // NQ, G])
        stats = sb("stats", [P, NT, 6])
        mv = sb("mv", [P, NTT, 2])
        ve = sb("ve", [P, NTT])
        sd = sb("sd", [P, NTT])
        rc = sb("rc", [P, NTT])
        nw = sb("nw", [P, NTT])
        rstd = sb("rstd", [P, NTT])
        xn = sb("xn", [P, 2, NT, D])
        t1, t2 = (probs[:, i, :, :].rearrange("p (s a) c -> p s (a c)", s=2) for i in range(2))
        rot, res = (ctx_all[:, i * NG // 2:(i + 1) * NG // 2, :].rearrange("p (s a) c -> p s (a c)", s=2)
                    for i in range(2))
        part = sb("part", [P, 2, PARTS, T], BF16)
        v_T = sb("v_T", [P, T])
        stage = xn[:, 0, :, :]
        ctx_T = v_T
        out_sb = sb("out_sb", [P, 2, NT, D])

        s_ps = ctx.enter_context(nc.psum_tensor("s_ps", [P, SLOTS, 2, W], F32))
        acc_ps = ctx.enter_context(nc.psum_tensor("acc_ps", [P, W], F32))
        a_ps = ctx.enter_context(nc.psum_tensor("a_ps", [P, RING, W], F32))
        neg_ps = a_ps[:, 0, :].bitcast(BF16)

        x_in = [sem(f"x_in{b}") for b in range(B)]
        const_in = sem("const_in")
        ffn_in = sem("ffn_in")
        zeroed = sem("zeroed")
        stat = sem("stat")
        sd_done = sem("sd_done")
        rstd_done = sem("rstd_done")
        xn_done = sem("xn_done")
        xnt_ps = sem("xnt_ps")
        xnt_done = sem("xnt_done")
        proj_ps = sem("proj_ps")
        rope_mul = sem("rope_mul")
        rope_sum = sem("rope_sum")
        part_hi = sem("part_hi")
        part_res = sem("part_res")
        part_mid = sem("part_mid")
        part_lo = sem("part_lo")
        parts_stored = [sem(f"parts_stored{i}") for i in range(2)]
        vt_ps = sem("vt_ps")
        vt_done = sem("vt_done")
        v_ps = sem("v_ps")
        v_done = sem("v_done")
        ones_done = sem("ones_done")
        w_done = sem("w_done")
        id_done = sem("id_done")
        bo_added = sem("bo_added")
        qa_loaded = [sem(f"qa_loaded{i}") for i in range(2)]
        qc_loaded = [sem(f"qc_loaded{i}") for i in range(2)]
        v_grp_done = sem("v_grp_done")
        a_ready = sem("a_ready")
        max_done = sem("max_done")
        neg_step = sem("neg_step")
        neg_T_ps = sem("neg_T_ps")
        neg_T_done = sem("neg_T_done")
        neg_loaded = sem("neg_loaded")
        scores_ready = sem("scores_ready")
        exp_done = sem("exp_done")
        pv_done = sem("pv_done")
        acc_copied = sem("acc_copied")
        ffn_up = sem("ffn_up")
        tanh_done = sem("tanh_done")
        gated_done = sem("gated_done")
        hid_done = sem("hid_done")
        ffn_down = sem("ffn_down")
        y_done = sem("y_done")
        ctx_ps = sem("ctx_ps")
        rec_done = sem("rec_done")
        normed = sem("normed")
        staged = sem("staged")
        ctx_T_ps = sem("ctx_T_ps")
        ctx_T_done = sem("ctx_T_done")
        o_ps = sem("o_ps")
        o_done = sem("o_done")
        out_stored = [sem(f"out_stored{i}") for i in range(2)]

        NEG = 5
        SLICES = B + 1
        block = ctx.enter_context(nc.Block())

        @block.sync
        def _(sp):
            for b in range(B):
                sp.dma_start(y_all[:, b * NT:(b + 1) * NT, :],
                             x[b].rearrange("(t p) d -> p t d", p=P)).then_inc(x_in[b], 16)

            def store_parts(s):
                sp.wait_ge(part_lo, s + 1)
                for n in range(PARTS):
                    if s < B:
                        for k in range(KV):
                            sp.dma_start(q_parts[s * KV + k, n * HD:(n + 1) * HD].rearrange("d j t -> j d t"),
                                         part[k * G * HD:(k + 1) * G * HD, s % 2, n, :]).then_inc(parts_stored[s % 2], 16)
                    else:
                        sp.dma_start(k_parts[:, n, :, :], part[:, s % 2, n, :]).then_inc(parts_stored[s % 2], 16)

            for s in range(SLICES):
                store_parts(s)
            sp.wait_ge(parts_stored[0], 16 * PARTS * (KV * B // 2 + 1))
            sp.wait_ge(parts_stored[1], 16 * PARTS * KV * B // 2)
            sp.wait_ge(zeroed, 10)

            def load_parts(g, q_buf, k_buf, loaded):
                R = PARTS * HD
                for c in range(PARTS):
                    sp.dma_start(q_buf[c * R:(c + 1) * R, :, :], q_parts[g]).then_inc(loaded, 16)
                for n in range(PARTS):
                    sp.dma_start(k_buf[n * R:(n + 1) * R, :],
                                 k_parts[g, n].unsqueeze(0).to_broadcast([PARTS, HD, T])).then_inc(loaded, 16)

            def load_neg(g, par):
                sp.wait_ge(neg_T_done, g + 1)
                for n in range(PARTS):
                    sp.dma_start(qc[par][MAX_ROW + n:MAX_ROW + n + 1, :, :],
                                 neg_max_T[n * G * NT:(n + 1) * G * NT, :]).then_inc(neg_loaded, 16)

            load_parts(0, qa[0], ka[0], qa_loaded[0])
            load_parts(1, qa[1], ka[1], qa_loaded[1])
            load_parts(0, qc[0], kc[0], qc_loaded[0])
            load_neg(0, 0)

            def group(g, par, left):
                if left > 1:
                    sp.wait_ge(pv_done, STEPS * g + SLOTS)
                    load_parts(g + 1, qc[1 - par], kc[1 - par], qc_loaded[1 - par])
                if left > 2:
                    sp.wait_ge(a_ready, AU * (g + 1))
                    load_parts(g + 2, qa[par], ka[par], qa_loaded[par])
                if left > 1:
                    load_neg(g + 1, 1 - par)

            with sp.Fori(0, NG // 2 - 1) as pair:
                group(pair * 2, 0, 3)
                group(pair * 2 + 1, 1, 3)
            group(NG - 2, 0, 2)
            group(NG - 1, 1, 1)

            for b in range(B):
                sp.wait_ge(o_done, b + 1)
                sp.dma_start(out[b].rearrange("(t p) d -> p t d", p=P), out_sb[:, b % 2, :, :])\
                    .then_inc(out_stored[b % 2], 16)
            for i in range(2):
                sp.wait_ge(out_stored[i], 16 * B // 2)

        @block.gpsimd
        def _(pool):
            for i in range(2):
                for t in (qa[i][:, :, :], qc[i][:, :, :], ka[i][:, :], kc[i][:, :]):
                    nc.gpsimd.memset(t[64:P], 0.0).then_inc(zeroed, 1)
            pool.wait_ge(zeroed, 8)
            for i in range(2):
                nc.gpsimd.memset(kc[i][MAX_ROW:MAX_ROW + PARTS, :], 1.0).then_inc(zeroed, 1)
            pool.wait_ge(zeroed, 10)

            for s in range(SLICES):
                i = s % 2
                pool.wait_ge(rope_mul, 2 * (s + 1))
                if s >= 2:
                    pool.wait_ge(part_res, s - 1)
                    pool.wait_ge(part_hi, s - 1)
                nc.gpsimd.tensor_tensor(rot[:, i, :], t1[:, i, :], t2[:, i, :], ALU.add).then_inc(rope_sum, 1)
                pool.wait_ge(rope_sum, s + 1)
                pool.wait_ge(part_hi, s + 1)
                nc.gpsimd.tensor_tensor(res[:, i, :], rot[:, i, :], part[:, i, 0, :],
                                        ALU.subtract).then_inc(part_res, 1)
                pool.wait_ge(part_res, s + 1)
                pool.wait_ge(part_mid, s + 1)
                nc.gpsimd.tensor_tensor(part[:, i, 2, :], res[:, i, :], part[:, i, 1, :],
                                        ALU.subtract).then_inc(part_lo, 1)
                pool.wait_ge(part_lo, s + 1)
            for b in range(B):
                pool.wait_ge(xn_done, b + 1)
                nc.gpsimd.tensor_tensor(y_all[:, b * NT:(b + 1) * NT, :], y_all[:, b * NT:(b + 1) * NT, :],
                                        bo_sb[:, :].unsqueeze(1).to_broadcast([P, NT, D]), ALU.add).then_inc(bo_added, 1)

            pool.wait_ge(ones_done, 2)
            pool.wait_ge(v_done, 1)

            def copy_v(g, par):
                nc.gpsimd.tensor_copy(v_grp[par][:, :, 0:HD], v_all[:, :, g, :]).then_inc(v_grp_done, 1)

            copy_v(0, 0)

            def group(g, par):
                pool.wait_ge(pv_done, STEPS * g + SLOTS)
                copy_v(g + 1, 1 - par)

            with pool.Fori(0, NG // 2 - 1) as pair:
                group(pair * 2, 0)
                group(pair * 2 + 1, 1)
            group(NG - 2, 0)

        @block.scalar
        def _(act):
            act.dma_start(wf_sb[:, :], wf).then_inc(const_in, 16)
            act.dma_start(ident[:, :], identity).then_inc(const_in, 16)
            act.dma_start(bias_sb[:, :], biases).then_inc(const_in, 16)
            act.dma_start(rope[:, :, :], tables).then_inc(const_in, 16)
            act.dma_start(bo_sb[:, :], bo.partition_broadcast(P)).then_inc(const_in, 16)
            act.dma_start(wi_sb[:, :], wi).then_inc(ffn_in, 16)
            act.sem_inc(exp_done, SLOTS)
            act.sem_inc(acc_copied, 1)
            for b in range(B):
                act.wait_ge(stat, b + 1)
                nc.scalar.activation(sd[:, b * NT:(b + 1) * NT], ve[:, b * NT:(b + 1) * NT], ACT.Sqrt)\
                    .then_inc(sd_done, 1)
            nc.scalar.preload_act_table(ACT.Exp)

            def split(s):
                i = s % 2
                if s >= 2:
                    act.wait_ge(parts_stored[i], 16 * PARTS * KV * (s // 2))
                act.wait_ge(rope_sum, s + 1)
                nc.scalar.activation(part[:, i, 0, :], rot[:, i, :], ACT.Copy).then_inc(part_hi, 1)
                act.wait_ge(part_res, s + 1)
                nc.scalar.activation(part[:, i, 1, :], res[:, i, :], ACT.Copy).then_inc(part_mid, 1)

            for b in range(B):
                for h in range(2):
                    act.wait_ge(xnt_ps, 2 * b + h + 1)
                    nc.scalar.activation(xn_T[:, b * T + h * W:b * T + (h + 1) * W], a_ps[:, h, :],
                                         ACT.Copy).then_inc(xnt_done, 1)
                if b >= 1:
                    split(b - 1)
            split(B - 1)
            split(B)
            act.wait_ge(vt_ps, 1)
            nc.scalar.activation(v_T[:, :], s_ps[:, 0, :, :], ACT.Identity, bias=bias_sb[:, 4:5]).then_inc(vt_done, 1)
            act.wait_ge(v_ps, 1)
            nc.scalar.activation(v_all[:, :, :, :], a_ps[:, 0:2, :], ACT.Copy).then_inc(v_done, 1)

            def copy_neg(g):
                act.wait_ge(neg_T_ps, g + 1)
                nc.scalar.activation(neg_max_T[:, :], neg_ps[0:PARTS * G * NT, 0:P], ACT.Copy).then_inc(neg_T_done, 1)

            copy_neg(0)

            def copy_acc(g, h):
                act.wait_ge(pv_done, STEPS * g + NT * (h + 1) + SLOTS)
                nc.scalar.activation(acc_sb[:, h, :], acc_ps[:, :], ACT.Copy).then_inc(acc_copied, 1)

            def group(g, left):
                for s in range(STEPS):
                    act.wait_ge(pv_done, STEPS * g + s + 1)
                    for u in range(UNITS):
                        act.wait_ge(scores_ready, UNITS * (STEPS * g + s) + u + 1)
                        nc.scalar.activation(probs[:, s % SLOTS, 2 * u:2 * u + 2, :], s_ps[:, u, :, :], ACT.Exp,
                                             scale=SCALE).then_inc(exp_done, 1)
                    if s == NT:
                        copy_acc(g, 0)
                if left > 1:
                    copy_neg(g + 1)
                for c in range(FC):
                    act.wait_ge(ffn_up, FC * g + c + 1)
                    nc.scalar.activation(th[:, c, :], a_ps[:, (1 + c) % RING, 0:CH], ACT.Tanh,
                                         scale=0.5).then_inc(tanh_done, 1)
                copy_acc(g, 1)

            with act.Fori(0, NG // 2 - 1) as pair:
                group(pair * 2, 3)
                group(pair * 2 + 1, 3)
            group(NG - 2, 2)
            group(NG - 1, 1)

            act.wait_ge(normed, 2 * NG + 1)
            for b in range(B):
                if b >= 1:
                    act.wait_ge(ctx_T_ps, 2 * b)
                nc.scalar.activation(stage[:, :, :].rearrange("p t (k c) -> p k t c", k=KV),
                                     ctx_all[:, b * KV:(b + 1) * KV, :].rearrange("p k (t c) -> p k t c", t=NT),
                                     ACT.Copy).then_inc(staged, 1)

        @block.vector
        def _(dve):
            dve.sem_inc(normed, 1)

            def norm(b):
                tiles = slice(b * NT, (b + 1) * NT)
                dve.wait_ge(x_in[b], 16)
                for t in range(NT):
                    last = nc.vector.bn_stats(stats[:, t, :], y_all[:, b * NT + t, :])
                dve.drain()
                for t in range(NT):
                    nc.vector.bn_aggr(mv[:, b * NT + t, :], stats[:, t, :])
                dve.drain()
                nc.vector.tensor_scalar(ve[:, tiles], mv[:, tiles, 1], EPS, None, ALU.add).then_inc(stat, 1)

            def root(b):
                tiles = slice(b * NT, (b + 1) * NT)
                dve.wait_ge(sd_done, b + 1)
                nc.vector.reciprocal(rc[:, tiles], sd[:, tiles])
                dve.drain()
                nc.vector.tensor_tensor(nw[:, tiles], ve[:, tiles], rc[:, tiles], ALU.mult)
                dve.drain()
                nc.vector.tensor_tensor(nw[:, tiles], nw[:, tiles], rc[:, tiles], ALU.mult)
                dve.drain()
                nc.vector.tensor_scalar(nw[:, tiles], nw[:, tiles], -0.5, 1.5, ALU.mult, ALU.add)
                dve.drain()
                nc.vector.tensor_tensor(rstd[:, tiles], nw[:, tiles], rc[:, tiles], ALU.mult)
                dve.drain()
                if b >= 2:
                    dve.wait_ge(xnt_ps, 2 * (b - 1))
                for t in range(NT):
                    n = b * NT + t
                    last = nc.vector.tensor_scalar(xn[:, b % 2, t, :], y_all[:, n, :], mv[:, n, 0:1], rstd[:, n:n + 1],
                                                   ALU.subtract, ALU.mult)
                last.then_inc(xn_done, 1)

            def rotate(s):
                i = s % 2
                col = 0 if s < B else 2
                if s >= 2:
                    dve.wait_ge(rope_sum, s - 1)
                for n, dst in enumerate((t1, t2)):
                    dve.wait_ge(proj_ps, 2 * s + n + 1)
                    nc.vector.scalar_tensor_tensor(dst[:, i, :], s_ps[:, n, :, :].rearrange("p a c -> p (a c)"), bias_sb[:, col + n:col + n + 1],
                                                   rope[:, n, :], ALU.add, ALU.mult).then_inc(rope_mul, 1)

            for i in range(2):
                nc.vector.memset(v_grp[i][:, :, :], 0.0)
            dve.drain()
            for i in range(2):
                nc.vector.memset(v_grp[i][:, :, HD:HD + 1], 1.0).then_inc(ones_done, 1)
            for b in range(B):
                norm(b)
            dve.wait_ge(const_in, 80)
            nc.vector.tensor_copy(ident16[:, :], ident[:, :]).then_inc(id_done, 1)
            for b in range(B):
                root(b)
                if b >= 1:
                    rotate(b - 1)
            rotate(B - 1)
            rotate(B)
            dve.wait_ge(ffn_in, 16)
            nc.vector.tensor_scalar(w_ffn[:, :], wi_sb[:, :], DEQUANT, None, ALU.mult).then_inc(w_done, 1)

            def reduce_max(g, a):
                dve.wait_ge(a_ready, AU * g + a + 1)
                nc.vector.tensor_reduce(out=mx[:, a // NQ, a % NQ:a % NQ + 1], in_=a_ps[:, a % RING, :], op=ALU.max,
                                        axis=AX.X).then_inc(max_done, 1)

            def split_neg(g):
                dve.wait_ge(max_done, AU * (g + 1))
                nc.vector.tensor_tensor(row_max[:, :], mx[:, :, 0], mx[:, :, 1], ALU.max).then_inc(neg_step, 1)
                dve.wait_ge(neg_step, NEG * g + 1)
                nc.vector.tensor_scalar(neg_max[:, 0, :], row_max[:, :], -1.0, None, ALU.mult).then_inc(neg_step, 1)
                dve.wait_ge(neg_step, NEG * g + 2)
                nc.vector.scalar_tensor_tensor(rest[:, :], row_max[:, :], -1.0, neg_max[:, 0, :], ALU.mult,
                                               ALU.subtract).then_inc(neg_step, 1)
                dve.wait_ge(neg_step, NEG * g + 3)
                nc.vector.tensor_copy(neg_max[:, 1, :], rest[:, :]).then_inc(neg_step, 1)
                dve.wait_ge(neg_step, NEG * g + 4)
                nc.vector.tensor_tensor(neg_max[:, 2, :], rest[:, :], neg_max[:, 1, :],
                                        ALU.subtract).then_inc(neg_step, 1)

            for a in range(AU):
                reduce_max(0, a)
            split_neg(0)
            dve.wait_ge(bo_added, B)

            def group(g, left):
                if left > 1:
                    for a in range(AU):
                        reduce_max(g + 1, a)
                    split_neg(g + 1)
                for c in range(FC):
                    bank = (1 + c) % RING
                    dve.wait_ge(tanh_done, FC * g + c + 1)
                    nc.vector.scalar_tensor_tensor(gated[:, c, :], th[:, c, :], 1.0, a_ps[:, bank, 0:CH], ALU.add,
                                                   ALU.mult).then_inc(gated_done, 1)
                    dve.wait_ge(gated_done, FC * g + c + 1)
                    nc.vector.scalar_tensor_tensor(hid[:, c, :], gated[:, c, :], 0.5, a_ps[:, bank, CH:2 * CH],
                                                   ALU.mult, ALU.mult).then_inc(hid_done, 1)
                dve.wait_ge(ffn_down, g + 1)
                chunk = y_all[:, bass.ds(g * CT, CT), :]
                nc.vector.tensor_tensor(chunk, chunk, a_ps[:, 1, 0:CT * D].rearrange("p (t d) -> p t d", t=CT),
                                        ALU.add).then_inc(y_done, 1)
                for h in range(NQ):
                    ps = a_ps[:, (2, 0)[h], :].rearrange("p (t j c) -> p t j c", t=NT // NQ, j=G)
                    dve.wait_ge(ctx_ps, NQ * g + h + 1)
                    nc.vector.reciprocal(rec[:, h, :, :], ps[:, :, :, HD]).then_inc(rec_done, 1)
                    dve.wait_ge(rec_done, NQ * g + h + 1)
                    cols = NT // NQ * G * HD
                    nc.vector.tensor_tensor(
                        ctx_all[:, g, h * cols:(h + 1) * cols].rearrange("p (t j d) -> p t j d", t=NT // NQ, j=G),
                        ps[:, :, :, 0:HD], rec[:, h, :, :].unsqueeze(3).to_broadcast([P, NT // NQ, G, HD]),
                        ALU.mult).then_inc(normed, 1)

            with dve.Fori(0, NG // 2 - 1) as pair:
                group(pair * 2, 3)
                group(pair * 2 + 1, 3)
            group(NG - 2, 2)
            group(NG - 1, 1)

            for b in range(B):
                for h in range(2):
                    dve.wait_ge(ctx_T_ps, 2 * b + h + 1)
                    nc.vector.tensor_copy(ctx_T[:, h * W:(h + 1) * W], s_ps[:, 0, h, :]).then_inc(ctx_T_done, 1)
                dve.wait_ge(o_ps, b + 1)
                if b >= 2:
                    dve.wait_ge(out_stored[b % 2], 16 * (b // 2))
                nc.vector.tensor_tensor(out_sb[:, b % 2, :, :], y_all[:, b * NT:(b + 1) * NT, :],
                                        s_ps[:, 1, :, :].rearrange("p a (t d) -> p (a t) d", d=D),
                                        ALU.add).then_inc(o_done, 1)

        @block.tensor
        def _(pe):
            pe.sem_inc(pv_done, SLOTS)
            pe.wait_ge(const_in, 80)

            def transpose_xn(b):
                pe.wait_ge(xn_done, b + 1)
                if b >= 1:
                    pe.wait_ge(xnt_done, 2 * b)
                for t in range(NT):
                    last = nc.tensor.transpose(a_ps[:, t // 4, t % 4 * P:(t % 4 + 1) * P], xn[:, b % 2, t, :],
                                               ident[:, :])
                    if t % 4 == 3:
                        last.then_inc(xnt_ps, 1)

            def project(b):
                pe.wait_ge(xnt_done, 2 * (b + 1))
                for n, c in enumerate((C_Q, C_QR)):
                    if b >= 1:
                        pe.wait_ge(rope_mul, 2 * (b - 1) + n + 1)
                    for h in range(2):
                        last = nc.tensor.matmul(s_ps[:, n, h, :], wf_sb[:, c:c + D],
                                                xn_T[:, b * T + h * W:b * T + (h + 1) * W], start=True, stop=True)
                    last.then_inc(proj_ps, 1)

            def project_kv(dst, c):
                for h in range(2):
                    for b in range(B):
                        last = nc.tensor.matmul(dst[32 * b:32 * b + 32, h, :], wf_sb[:, c:c + 32],
                                                xn_T[:, b * T + h * W:b * T + (h + 1) * W], start=True, stop=True,
                                                )
                return last

            for b in range(B):
                transpose_xn(b)
                if b >= 1:
                    project(b - 1)
            project(B - 1)
            for n, c in enumerate((C_K, C_KR)):
                pe.wait_ge(rope_mul, 2 * (B - 1) + n + 1)
                project_kv(s_ps[:, n, :, :], c).then_inc(proj_ps, 1)
            pe.wait_ge(rope_mul, 2 * B + 1)
            project_kv(s_ps[:, 0, :, :], C_V).then_inc(vt_ps, 1)
            pe.wait_ge(vt_done, 1)
            for t in range(NT):
                last = nc.tensor.transpose(a_ps[:, t // 4, t % 4 * P:(t % 4 + 1) * P], v_T[:, t * P:(t + 1) * P],
                                           ident[:, :])
            last.then_inc(v_ps, 1)
            pe.wait_ge(v_done, 1)
            pe.wait_ge(id_done, 1)
            pe.wait_ge(w_done, 1)

            def max_unit(g, par, a):
                j, t, h = a // (NT * NQ), a // NQ % NT, a % NQ
                if a >= RING:
                    pe.wait_ge(max_done, AU * g + a - RING + 1)
                nc.tensor.matmul(a_ps[:, a % RING, :], qa[par][0:MAX_ROW, j, t * P:(t + 1) * P],
                                 ka[par][0:MAX_ROW, h * W:(h + 1) * W], start=True, stop=True).then_inc(a_ready, 1)

            def transpose_neg(g):
                pe.wait_ge(neg_step, NEG * (g + 1))
                nc.tensor.transpose(neg_ps[0:PARTS * G * NT, 0:P], neg_max[:, :, :], ident16[:, :])\
                    .then_inc(neg_T_ps, 1)

            DMAS = 16 * 2 * PARTS
            pe.wait_ge(qa_loaded[0], DMAS)
            for a in range(AU):
                max_unit(0, 0, a)
            transpose_neg(0)

            def scores(g, par, s, u):
                kt, h = s % NT, s // NT
                pe.wait_ge(exp_done, UNITS * (STEPS * g + s) + u + 1)
                for i in range(2):
                    last = nc.tensor.matmul(s_ps[:, u, i, :], kc[par][:, kt * P:(kt + 1) * P],
                                            qc[par][:, 2 * u + i, h * W:(h + 1) * W], start=True, stop=True)
                last.then_inc(scores_ready, 1)

            def weigh(g, par, s):
                kt, h = s % NT, s // NT
                if kt == 0:
                    pe.wait_ge(acc_copied, NQ * g + h + 1)
                pe.wait_ge(exp_done, UNITS * (STEPS * g + s + 1) + SLOTS)
                for j in range(G):
                    last = nc.tensor.matmul(acc_ps[VC * j:VC * (j + 1), :], v_grp[par][:, kt, :],
                                            probs[:, s % SLOTS, j, :], start=(kt == 0), stop=(kt == NT - 1))
                last.then_inc(pv_done, 1)

            def ffn_gate_up(g, c):
                bank = (1 + c) % RING
                for n in range(2):
                    last = nc.tensor.matmul(a_ps[:, bank, n * CH:(n + 1) * CH],
                                            w_ffn[:, n * HID + c * P:n * HID + (c + 1) * P],
                                            xn_T[:, bass.ds(g * CH, CH)], start=True, stop=True)
                last.then_inc(ffn_up, 1)

            def group(g, pair, par, left):
                pe.wait_ge(qc_loaded[par], (pair + 1) * DMAS)
                pe.wait_ge(v_grp_done, g + 1)
                pe.wait_ge(neg_loaded, (g + 1) * 16 * PARTS)
                scores(g, par, 0, 0)
                scores(g, par, 0, 1)
                if left > 1:
                    if par == 0:
                        pe.wait_ge(qa_loaded[1], (pair + 1) * DMAS)
                    else:
                        pe.wait_ge(qa_loaded[0], (pair + 2) * DMAS)
                pe.wait_ge(neg_T_done, g + 1)
                pe.wait_ge(normed, NQ * g + 1)
                a = 0
                for s in range(STEPS):
                    todo = A_OF[s] if left > 1 else 0
                    for u in range(UNITS):
                        if u < todo:
                            max_unit(g + 1, 1 - par, a)
                            a += 1
                        if s + 1 < STEPS:
                            scores(g, par, s + 1, u)
                    if s + 1 == STEPS:
                        if left > 1:
                            transpose_neg(g + 1)
                        ffn_gate_up(g, 0)
                        ffn_gate_up(g, 1)
                    for _ in range(UNITS, todo - 1):
                        max_unit(g + 1, 1 - par, a)
                        a += 1
                    weigh(g, par, s)
                    if todo > UNITS:
                        max_unit(g + 1, 1 - par, a)
                        a += 1
                assert left == 1 or a == AU
                if left > 1:
                    pe.wait_ge(neg_T_done, g + 2)
                ffn_gate_up(g, 2)
                pe.wait_ge(hid_done, FC * (g + 1))
                for t in range(CT):
                    for c in range(FC):
                        last = nc.tensor.matmul(a_ps[:, 1, t * D:(t + 1) * D], hid[:, c, t * P:(t + 1) * P],
                                                w_ffn[:, 2 * HID + c * D:2 * HID + (c + 1) * D],
                                                start=(c == 0), stop=(c == FC - 1))
                last.then_inc(ffn_down, 1)
                for h in range(NQ):
                    pe.wait_ge(acc_copied, NQ * g + h + 2)
                    for t in range(NT // NQ):
                        last = nc.tensor.transpose(a_ps[:, (2, 0)[h], t * P:(t + 1) * P],
                                                   acc_sb[:, h, t * P:(t + 1) * P], ident[:, :])
                    last.then_inc(ctx_ps, 1)

            with pe.Fori(0, NG // 2 - 1) as pair:
                group(pair * 2, pair, 0, 3)
                group(pair * 2 + 1, pair, 1, 3)
            group(NG - 2, NG // 2 - 1, 0, 2)
            group(NG - 1, NG // 2 - 1, 1, 1)

            for b in range(B):
                pe.wait_ge(staged, b + 1)
                for t in range(NT):
                    last = nc.tensor.transpose(s_ps[:, 0, t // 4, t % 4 * P:(t % 4 + 1) * P], stage[:, t, :],
                                               ident[:, :])
                    if t % 4 == 3:
                        last.then_inc(ctx_T_ps, 1)
                pe.wait_ge(ctx_T_done, 2 * (b + 1))
                if b >= 1:
                    pe.wait_ge(o_done, b)
                for t in range(NT):
                    last = nc.tensor.matmul(s_ps[:, 1, t // 4, t % 4 * D:(t % 4 + 1) * D],
                                            ctx_T[:, t * P:(t + 1) * P], wf_sb[:, C_O:C_O + D],
                                            start=True, stop=True)
                last.then_inc(o_ps, 1)


_INS = ["x", "wf", "wi", "biases", "bo", "tables", "identity"]


def kernel(**inputs):
    import numpy as np
    import concourse.bacc as bacc
    from concourse.bass_utils import run_bass_kernel_spmd

    p = "L0_attn_"
    a = {k: np.asarray(v) for k, v in inputs.items()}
    half = [1, 3, 5, 7, 0, 2, 4, 6]
    q_rows = [h * HD + r for h in range(H) for r in half]
    k_rows = [h * HD + r for h in range(KV) for r in half]
    wq, wk, wv, wo = (a[p + n] for n in ("Wq", "Wk", "Wv", "Wo"))
    bq, bk, bv = (a[p + n] for n in ("bq", "bk", "bv"))
    wf = np.concatenate([wq.T, wq[q_rows].T, wk.T, wk[k_rows].T, wv.T, wo.T], axis=1)
    down = a["L0_ffn_w_down"].T.reshape(FC, P, D).transpose(1, 0, 2).reshape(P, FC * D)
    wi = np.concatenate([a["L0_ffn_w_gate"].T, a["L0_ffn_w_up"].T, down], axis=1)
    biases = np.stack([bq, bq[q_rows], np.tile(bk, B), np.tile(bk[k_rows], B), np.tile(bv, B)], axis=1)
    freq = (np.float32(1.0) / np.float32(10000.0) ** (np.arange(0, HD, 2, dtype=np.float32) / np.float32(HD)))
    angle = np.arange(T, dtype=np.float32)[None, :] * freq.astype(np.float32)[:, None]
    cos = np.tile(np.cos(angle), (P // len(freq), 1))
    sin = np.tile(np.concatenate([-np.sin(angle), np.sin(angle)], axis=0), (P // HD, 1))
    tables = np.stack([cos, sin], axis=1).astype(np.float32)

    arrays = {
        "x": a[p + "hidden_states"], "wf": wf, "wi": wi, "biases": biases, "bo": a[p + "bo"], "tables": tables,
        "identity": np.eye(P, dtype=np.float32),
    }
    nc = bacc.Bacc("TRN2", target_bir_lowering=False, num_devices=1)
    arrays = {f"in_{n}": np.ascontiguousarray(arrays[n]) for n in _INS}
    aps = [nc.dram_tensor(n, v.shape, mybir.dt.from_np(v.dtype), kind="ExternalInput").ap() for n, v in arrays.items()]
    out = nc.dram_tensor("out_0", (B, T, D), F32, kind="ExternalOutput").ap()
    attention_swiglu(nc, *aps, out)
    r = run_bass_kernel_spmd(nc, [arrays], core_ids=[0])
    return r.results[0]["out_0"]
```

```python
from contextlib import ExitStack

import concourse.bass as bass
from concourse import mybir

F32 = mybir.dt.float32
BF16 = mybir.dt.bfloat16
I32 = mybir.dt.int32
ALU = mybir.AluOpType
ACT = mybir.ActivationFunctionType
AX = mybir.AxisListType

B, T, D = 4, 1024, 128
H, G = 16, 4
HD = D // H
KV = H // G
HID = 384
P = 128
W = 512
NT = T // P
NTT = B * NT
NG = B * KV
PARTS = 3
ROWS = PARTS * HD
MAX_ROW = 96
NH = T // W
HT = NT // NH
STEPS = NH * NT
SLOTS = 2
HU = G * HT * 2
AU = NH * HU
PER = AU // STEPS
LEAD = 48
S_BANKS = 3
RING = 4
FIRST_RING = 3
SG = G * STEPS
CH = T * B // NG
CT = CH // P
FC = HID // P
VC = 32
SCALE = HD ** -0.5
DEQUANT = 1.0 / 127.0
EPS = 1e-5
C_S0, C_Q, C_K = 0, 2 * D, 4 * D
C_V = C_K + 2 * 32
C_O = C_V + 32
C_ALL = C_O + D
B_S0, B_S1, B_Q, B_V = 0, 2, 4, 6
FIRST, SECOND = 0, 1
Q_ROWS = P - HD * KV
PE_XN, PE_S1, PE_V, PE_VT, PE_Q = (0, 1, 3, 4), (5, 6, 7, 9), (11, 13), (15, 16), tuple(range(18, 42, 2))
DVE_S1 = (8, 11)
NEG_BEHIND = HU + 5
MAX, UP, DOWN, NEG_T, CTX, STAGE, PROJ = "max", "up", "down", "neg_T", "ctx", "stage", "proj"
JOB_AT = {1: (UP, 0), 3: (UP, 1), 5: (NEG_T, 1), 7: (UP, 2), 8: (CTX, 0), 10: (DOWN, 0), 13: (NEG_T, 0), 16: (CTX, 1)}
OUT_AT = 5
OUTS = 2 * B


def step_order(s, last_group):
    if last_group:
        units = [(MAX, PER * s + LEAD + i) for i in range(PER) if PER * s + LEAD < AU]
        jobs = [JOB_AT[s]] if s in JOB_AT and JOB_AT[s] != (NEG_T, 0) else []
        jobs += [(PROJ, s - OUT_AT - 1)] if OUT_AT < s <= OUT_AT + OUTS - 2 else []
        jobs += [(STAGE, s - OUT_AT)] if OUT_AT <= s < OUT_AT + OUTS - 2 else []
    else:
        units = [(MAX, PER * s + LEAD + i) for i in range(PER)]
        jobs = [JOB_AT[s]] if s in JOB_AT else []
    return units[:3] + jobs + units[3:]


ORDER = [o for s in range(1, STEPS + 1) for o in step_order(s, False)]
LAST_ORDER = [o for s in range(1, STEPS) for o in step_order(s, True)]
LAST_ORDER += [JOB_AT[STEPS]] + [o for u in range(OUTS - 2, OUTS) for o in ((STAGE, u), (PROJ, u))]
assert len(ORDER) % RING == 0


def score_bank(u):
    return u % S_BANKS if u < SG - 1 else 1


def score_before(u):
    return max(v for v in range(-SG, u) if score_bank(v % SG) == score_bank(u))


def attention_swiglu(nc, x, wf, wi, biases, bo, tables, identity, out):
    q_parts = nc.dram_tensor("q_parts", (NG, G, HD, PARTS, T), BF16, kind="Internal").ap()
    k_parts = nc.dram_tensor("k_parts", (NG, HD, PARTS, T), BF16, kind="Internal").ap()

    with ExitStack() as ctx:
        def sb(name, shape, dt=F32):
            return ctx.enter_context(nc.sbuf_tensor(name, shape, dt))

        def sem(name):
            return ctx.enter_context(nc.semaphore(name))

        def sems(name, n=2):
            return [sem(f"{name}{i}") for i in range(n)]

        ident = sb("ident", [P, P])
        ident16 = sb("ident16", [P, P], BF16)
        wf_sb = sb("wf_sb", [P, C_ALL])
        wi_sb = sb("wi_sb", [P, 3 * HID], I32)
        w_ffn = sb("w_ffn", [P, 3 * HID])
        bias_sb = sb("bias_sb", [P, B_V + 1])
        bo_sb = sb("bo_sb", [P, D])
        rope = sb("rope", [P, 2, T])
        y_all = sb("y_all", [P, NTT, D])
        xn_T = sb("xn_T", [P, B * T])
        ctx_all = sb("ctx_all", [P, NG, NT * G * HD])
        v_all = sb("v_all", [P, NT, NG, HD])
        v_grp = [sb(f"v_grp{i}", [P, NT, VC]) for i in range(2)]
        qa = [sb(f"qa{i}", [P, G, T], BF16) for i in range(2)]
        ka = [sb(f"ka{i}", [P, T], BF16) for i in range(2)]
        qc = [sb(f"qc{i}", [P, NH, G, W], BF16) for i in range(2)]
        kc = [sb(f"kc{i}", [P, T], BF16) for i in range(2)]
        probs = sb("probs", [P, SLOTS, G, W])
        acc_sb = sb("acc_sb", [P, NH, W])
        mx = sb("mx", [P, NH, G * HT, 2])
        row_max = sb("row_max", [P, G * HT])
        rest = sb("rest", [P, G * HT])
        neg_max = sb("neg_max", [P, 2 * PARTS, G * HT], BF16)
        neg_max_T = sb("neg_max_T", [PARTS * G * HT, P], BF16)
        th = sb("th", [P, FC, CH])
        gated = sb("gated", [P, FC, CH])
        hid = sb("hid", [P, FC, CH])
        rec = sb("rec", [P, NH, HT, G])
        stats = sb("stats", [P, NTT, 6])
        mv = sb("mv", [P, NTT, 2])
        ve = sb("ve", [P, NTT])
        sd = sb("sd", [P, NTT])
        rc = sb("rc", [P, NTT])
        nw = sb("nw", [P, NTT])
        rstd = sb("rstd", [P, NTT])
        shift = sb("shift", [P, NTT])
        xn = sb("xn", [P, B, NT, D])
        t1, t2 = (probs[:, i, :, :].rearrange("p (s a) c -> p s (a c)", s=2) for i in range(2))
        rot, res = (ctx_all[:, i * NG // 2:(i + 1) * NG // 2, :].rearrange("p (s a) c -> p s (a c)", s=2)
                    for i in range(2))
        part = sb("part", [P, 2, PARTS, T], BF16)
        v_T = sb("v_T", [P, T])
        raw = [xn[:, 0:2, :, :], xn[:, 2:4, :, :], sb("raw", [P, 2, NT, D])]
        raw = [r.rearrange("p n t d -> p n (t d)") if i < 2 else r[:, :, :, :].rearrange("p n t d -> p n (t d)")
               for i, r in enumerate(raw)]
        stage = xn
        ctx_T = v_T

        acc_ps = ctx.enter_context(nc.psum_tensor("acc_ps", [P, W], F32))
        banks = ctx.enter_context(nc.psum_tensor("banks", [P, S_BANKS + RING, W], F32))
        s_ps = banks[:, 0:4, :].rearrange("p (n h) w -> p n h w", n=2)

        def bank(slot):
            return banks[:, S_BANKS + (slot + PER) % RING, :]

        def first_bank(slot):
            return banks[:, 4 + (slot - LEAD - 1) % FIRST_RING, :]

        def first_slot(a):
            return a + (a > NEG_BEHIND)

        x_in = sems("x_in", B)
        w_in = sem("w_in")
        const_in = sem("const_in")
        ffn_in = sem("ffn_in")
        zeroed = sem("zeroed")
        ones_done = sem("ones_done")
        stat = sem("stat")
        sd_done = sem("sd_done")
        newton = sem("newton")
        rstd_done = sem("rstd_done")
        xn_done = sem("xn_done")
        xn_done_pool = sem("xn_done_pool")
        xnt_ps = sem("xnt_ps")
        xnt_done = sem("xnt_done")
        proj_ps = sem("proj_ps")
        rope_mul = sem("rope_mul")
        rope_sum = sem("rope_sum")
        part_hi = sem("part_hi")
        part_res = sem("part_res")
        part_mid = sem("part_mid")
        part_lo = sem("part_lo")
        q_ps = sem("q_ps")
        raw_done = sem("raw_done")
        q_step = sem("q_step")
        q_dma = sem("q_dma")
        q_stored = sem("q_stored")
        parts_stored = sems("parts_stored")
        vt_ps = sem("vt_ps")
        vt_done = sem("vt_done")
        v_ps = sem("v_ps")
        v_done = sem("v_done")
        w_done = sem("w_done")
        id_done = sem("id_done")
        bo_added = sem("bo_added")
        qa_loaded = sems("qa_loaded")
        qc_loaded = sems("qc_loaded")
        v_grp_done = sem("v_grp_done")
        a_ready = sem("a_ready")
        max_done = sem("max_done")
        neg_step = sem("neg_step")
        neg_T_ps = sem("neg_T_ps")
        neg_T_done = sem("neg_T_done")
        neg_loaded = sem("neg_loaded")
        scores_ready = sem("scores_ready")
        exp_done = sem("exp_done")
        pv_done = sem("pv_done")
        acc_copied = sem("acc_copied")
        ffn_up = sem("ffn_up")
        tanh_done = sem("tanh_done")
        gated_done = sem("gated_done")
        hid_done = sem("hid_done")
        ffn_down = sem("ffn_down")
        y_done = sem("y_done")
        ctx_ps = sem("ctx_ps")
        rec_done = sem("rec_done")
        normed = sem("normed")
        staged = sem("staged")
        ctx_T_ps = sem("ctx_T_ps")
        ctx_T_done = sem("ctx_T_done")
        o_ps = sem("o_ps")
        o_done = sem("o_done")
        out_stored = sem("out_stored")

        NEG = 5
        Q_STEPS = 7
        DMAS = 16 * 2 * PARTS
        DMAS_C = 16 * (NH + 1) * PARTS
        block = ctx.enter_context(nc.Block())

        def context_half(g, h):
            cols = HT * G * HD
            return ctx_all[:, g, h * cols:(h + 1) * cols].rearrange("p (t j d) -> p t j d", t=HT, j=G)

        def normalise(eng, ops, b, done, halves=1):
            for t in range(NT):
                n = b * NT + t
                last = ops.tensor_scalar(xn[:, b, t, :], y_all[:, n, :], rstd[:, n:n + 1], shift[:, n:n + 1],
                                         ALU.mult, ALU.add)
                if (t + 1) % (NT // halves) == 0:
                    last.then_inc(done, 1)

        PIECES = [(FIRST, slice(0, W)), (FIRST, slice(W, T)), (SECOND, slice(0, T))]

        def rotate_sum(eng, ops, p):
            s, cols = PIECES[p]
            eng.wait_ge(rope_mul, 2 * (p + 1))
            ops.tensor_tensor(rot[:, s, cols], t1[:, s, cols], t2[:, s, cols], ALU.add).then_inc(rope_sum, 1)

        def residue(eng, ops, p):
            s, cols = PIECES[p]
            eng.wait_ge(rope_sum, p + 1)
            eng.wait_ge(part_hi, p + 1)
            ops.tensor_tensor(res[:, s, cols], rot[:, s, cols], part[:, s, 0, cols],
                              ALU.subtract).then_inc(part_res, 1)

        def low_part(eng, ops, p):
            s, cols = PIECES[p]
            eng.wait_ge(part_res, p + 1)
            eng.wait_ge(part_mid, p + 1)
            ops.tensor_tensor(part[:, s, 2, cols], res[:, s, cols], part[:, s, 1, cols],
                              ALU.subtract).then_inc(part_lo, 1)

        @block.sync
        def _(sp):
            for b in range(B):
                sp.dma_start(y_all[:, b * NT:(b + 1) * NT, :],
                             x[b].rearrange("(t p) d -> p t d", p=P)).then_inc(x_in[b], 16)

            def load_parts(g, q_buf, k_buf, loaded):
                for n in range(PARTS):
                    sp.dma_start(k_buf[n * ROWS:(n + 1) * ROWS, :],
                                 k_parts[g, :, n, :].unsqueeze(1).to_broadcast([HD, PARTS, T])).then_inc(loaded, 16)
                q_rows = q_parts[g].rearrange("j d n t -> (d n) j t")
                for c in range(PARTS):
                    if q_buf in qa:
                        sp.dma_start(q_buf[c * ROWS:(c + 1) * ROWS, :, :], q_rows).then_inc(loaded, 16)
                    else:
                        for h in range(NH):
                            sp.dma_start(q_buf[c * ROWS:(c + 1) * ROWS, h, :, :],
                                         q_rows[:, :, h * W:(h + 1) * W]).then_inc(loaded, 16)

            def load_neg(g, h, par):
                sp.wait_ge(neg_T_done, NH * g + h + 1)
                for n in range(PARTS):
                    sp.dma_start(qc[par][MAX_ROW + n:MAX_ROW + n + 1, h, :, :],
                                 neg_max_T[n * G * HT:(n + 1) * G * HT, :]).then_inc(neg_loaded, 16)

            sp.wait_ge(part_lo, 2)
            sp.dma_start(k_parts[0:KV].rearrange("g d n t -> (g d) n t"), part[Q_ROWS:P, FIRST, :, :])\
                .then_inc(parts_stored[0], 16)
            sp.dma_start(q_parts[0:KV - 1].rearrange("g j d n t -> (g j d) n t"), part[0:Q_ROWS, FIRST, :, :])\
                .then_inc(parts_stored[0], 16)
            sp.wait_ge(zeroed, 10)
            sp.wait_ge(parts_stored[0], 32)
            load_parts(0, qa[0], ka[0], qa_loaded[0])
            load_parts(0, qc[0], kc[0], qc_loaded[0])
            sp.wait_ge(part_lo, 3)
            sp.dma_start(q_parts[KV - 1].rearrange("j d n t -> (j d) n t"), part[0:P - Q_ROWS, SECOND, :, :])\
                .then_inc(parts_stored[1], 16)
            sp.dma_start(k_parts[KV:NG].rearrange("g d n t -> (g d) n t"), part[P - Q_ROWS:P, SECOND, :, :])\
                .then_inc(parts_stored[1], 16)
            sp.wait_ge(parts_stored[1], 32)
            load_parts(1, qa[1], ka[1], qa_loaded[1])
            load_neg(0, 0, 0)

            def group(g, par, left):
                if left > 1:
                    sp.wait_ge(pv_done, STEPS * g + SLOTS)
                    load_parts(g + 1, qc[1 - par], kc[1 - par], qc_loaded[1 - par])
                load_neg(g, 1, par)
                if left > 2:
                    sp.wait_ge(a_ready, AU * (g + 1))
                    load_parts(g + 2, qa[par], ka[par], qa_loaded[par])
                if left > 1:
                    load_neg(g + 1, 0, 1 - par)

            with sp.Fori(0, NG // 2 - 1) as pair:
                group(pair * 2, 0, 3)
                group(pair * 2 + 1, 1, 3)
            group(NG - 2, 0, 2)
            group(NG - 1, 1, 1)

            for u in range(OUTS):
                sp.wait_ge(o_done, u + 1)
                sp.dma_start(out[u // 2, (u % 2) * W:(u % 2 + 1) * W, :].rearrange("(t p) d -> p t d", p=P),
                             y_all[:, u * HT:(u + 1) * HT, :]).then_inc(out_stored, 16)
            sp.wait_ge(out_stored, 16 * OUTS)

        @block.gpsimd
        def _(pool):
            for i in range(2):
                for t in (qa[i][64:P].rearrange("p j t -> p (j t)"), qc[i][64:P].rearrange("p h j w -> p (h j w)")):
                    nc.gpsimd.memset(t.bitcast(F32), 0.0).then_inc(zeroed, 1)
                for t in (ka[i][:, :], kc[i][:, :]):
                    nc.gpsimd.memset(t[64:P].bitcast(F32), 0.0).then_inc(zeroed, 1)
            pool.wait_ge(zeroed, 8)
            for i in range(2):
                nc.gpsimd.memset(kc[i][MAX_ROW:MAX_ROW + PARTS, :], 1.0).then_inc(zeroed, 1)
            pool.wait_ge(zeroed, 10)
            pool.sem_inc(q_stored, 1)
            pool.wait_ge(rstd_done, 2)
            for b in (2, 3):
                normalise(pool, nc.gpsimd, b, xn_done_pool)
            rotate_sum(pool, nc.gpsimd, 2)
            residue(pool, nc.gpsimd, 2)
            low_part(pool, nc.gpsimd, 2)

            def copy_v(g, par):
                nc.gpsimd.tensor_copy(v_grp[par][:, :, 0:HD], v_all[:, :, g, :]).then_inc(v_grp_done, 1)

            pool.wait_ge(ones_done, 2)
            pool.wait_ge(v_done, 1)
            copy_v(0, 0)
            copy_v(1, 1)
            pool.wait_ge(xn_done, 4)
            for b in range(B):
                nc.gpsimd.tensor_tensor(y_all[:, b * NT:(b + 1) * NT, :], y_all[:, b * NT:(b + 1) * NT, :],
                                        bo_sb[:, :].unsqueeze(1).to_broadcast([P, NT, D]),
                                        ALU.add).then_inc(bo_added, 1)

            def split_q(b):
                i, n = (b - 1) % 2, Q_STEPS * (b - 1)
                q, twin = (raw[b - 1][:, k, :] for k in range(2))
                pool.wait_ge(raw_done, 2 * b)
                nc.gpsimd.tensor_tensor(q, q, rope[:, 0, :], ALU.mult).then_inc(q_step, 1)
                nc.gpsimd.tensor_tensor(twin, twin, rope[:, 1, :], ALU.mult).then_inc(q_step, 1)
                pool.wait_ge(q_step, n + 2)
                nc.gpsimd.tensor_tensor(q, q, twin, ALU.add).then_inc(q_step, 1)
                if b == 2:
                    pool.wait_ge(parts_stored[1], 32)
                pool.wait_ge(q_step, n + 3)
                nc.gpsimd.tensor_copy(part[:, i, 0, :], q).then_inc(q_step, 1)
                pool.wait_ge(q_step, n + 4)
                nc.gpsimd.tensor_tensor(twin, q, part[:, i, 0, :], ALU.subtract).then_inc(q_step, 1)
                pool.wait_ge(q_step, n + 5)
                nc.gpsimd.tensor_copy(part[:, i, 1, :], twin).then_inc(q_step, 1)
                pool.wait_ge(q_step, n + 6)
                nc.gpsimd.tensor_tensor(part[:, i, 2, :], twin, part[:, i, 1, :], ALU.subtract).then_inc(q_step, 1)
                pool.wait_ge(q_step, n + 7)
                pool.dma_start(q_parts[b * KV:(b + 1) * KV].rearrange("g j d n t -> (g j d) n t"),
                               part[:, i, :, :]).then_inc(q_dma, 16)
                pool.wait_ge(q_dma, 16 * b)
                pool.sem_inc(q_stored, 2)

            pool.wait_ge(parts_stored[0], 32)
            for b in range(1, B):
                split_q(b)

            def group(g, par):
                pool.wait_ge(pv_done, STEPS * (g + 1) + SLOTS)
                copy_v(g + 2, par)

            with pool.Fori(0, NG // 2 - 1) as pair:
                group(pair * 2, 0)
                group(pair * 2 + 1, 1)

            for u in range(OUTS):
                b = u // 2
                pool.wait_ge(normed, NH * KV * b + NH * (KV - 1) + u % 2 + 2)
                dst = stage[:, b, (u % 2) * HT:(u % 2 + 1) * HT, :].rearrange("p t (k c) -> p k t c", k=KV)
                half = slice((u % 2) * HT * G * HD, (u % 2 + 1) * HT * G * HD)
                src = ctx_all[:, b * KV:(b + 1) * KV, half].rearrange("p k (t c) -> p k t c", t=HT)
                nc.gpsimd.tensor_copy(dst, src).then_inc(staged, 1)

        @block.scalar
        def _(act):
            act.dma_start(ident[:, :], identity).then_inc(w_in, 16)
            act.dma_start(wf_sb[:, :], wf).then_inc(w_in, 16)
            act.dma_start(bias_sb[:, :], biases).then_inc(const_in, 16)
            act.dma_start(rope[:, :, :], tables).then_inc(const_in, 16)
            act.dma_start(bo_sb[:, :], bo.partition_broadcast(P)).then_inc(const_in, 16)
            act.dma_start(wi_sb[:, :], wi).then_inc(ffn_in, 16)
            act.sem_inc(exp_done, G)

            def root(tiles, n):
                act.wait_ge(stat, n)
                nc.scalar.activation(sd[:, tiles], ve[:, tiles], ACT.Sqrt).then_inc(sd_done, 1)

            def copy_xn_T(b):
                for h in range(2):
                    act.wait_ge(xnt_ps, 2 * b + h + 1)
                    nc.scalar.activation(xn_T[:, b * T + h * W:b * T + (h + 1) * W], (s_ps[:, 0, 0, :], acc_ps[:, :])[h],
                                         ACT.Copy).then_inc(xnt_done, 1)

            def split_high(p):
                s, cols = PIECES[p]
                act.wait_ge(rope_sum, p + 1)
                nc.scalar.activation(part[:, s, 0, cols], rot[:, s, cols], ACT.Copy).then_inc(part_hi, 1)

            def split_mid(p):
                s, cols = PIECES[p]
                act.wait_ge(part_res, p + 1)
                nc.scalar.activation(part[:, s, 1, cols], res[:, s, cols], ACT.Copy).then_inc(part_mid, 1)

            def copy_q(b, n):
                act.wait_ge(q_ps, 2 * (b - 1) + n + 1)
                nc.scalar.activation(raw[b - 1][:, n, :], s_ps[:, n, :, :].rearrange("p a c -> p (a c)"), ACT.Identity,
                                     bias=bias_sb[:, B_Q + n:B_Q + n + 1]).then_inc(raw_done, 1)

            def copy_neg(g, h, ps):
                act.wait_ge(neg_T_ps, NH * g + h + 1)
                nc.scalar.activation(neg_max_T[:, :], ps.bitcast(BF16)[0:PARTS * G * HT, 0:P],
                                     ACT.Copy).then_inc(neg_T_done, 1)

            def exps(g, s, heads):
                for j in heads:
                    if j == 0:
                        act.wait_ge(pv_done, STEPS * g + s + 1)
                    act.wait_ge(scores_ready, SG * g + G * s + j + 1)
                    nc.scalar.activation(probs[:, s % SLOTS, j, :], banks[:, score_bank(G * s + j), :], ACT.Exp,
                                         scale=SCALE).then_inc(exp_done, 1)

            root(slice(0, NT), 2 * NT + 1)
            copy_xn_T(0)
            split_high(0)
            split_high(1)
            split_mid(0)
            split_mid(1)
            root(slice(NT, NTT), 2 * NTT + 2)
            nc.scalar.preload_act_table(ACT.Exp)
            for b in range(1, B):
                copy_xn_T(b)
            act.wait_ge(const_in, 48)
            act.wait_ge(vt_ps, 1)
            nc.scalar.activation(v_T[:, :], s_ps[:, 0, :, :], ACT.Identity,
                                 bias=bias_sb[:, B_V:B_V + 1]).then_inc(vt_done, 1)
            split_high(2)
            act.wait_ge(v_ps, 1)
            nc.scalar.activation(v_all[:, :, :, :], s_ps[:, 1, :, :], ACT.Copy).then_inc(v_done, 1)
            split_mid(2)
            for b in range(1, B):
                copy_q(b, 0)
                if b == B - 1:
                    copy_neg(0, 0, first_bank(NEG_BEHIND + 1))
                copy_q(b, 1)
            act.wait_ge(rope_sum, 3)
            exps(0, 0, range(G))

            def group(g, left):
                slot = 0
                for s in range(1, STEPS + (left > 1)):
                    after = (g + (s + 1) // STEPS, (s + 1) % STEPS)
                    more = s + 1 < STEPS or left > 1
                    if more:
                        exps(*after, range(G - 1))
                    for kind, n in step_order(s, left == 1):
                        if kind == UP:
                            act.wait_ge(ffn_up, FC * g + n + 1)
                            nc.scalar.activation(th[:, n, :], bank(slot)[:, 0:CH], ACT.Tanh,
                                                 scale=0.5).then_inc(tanh_done, 1)
                        if kind == NEG_T:
                            copy_neg(g + 1 - n, n, bank(slot))
                        slot += 1
                    if more:
                        exps(*after, [G - 1])
                    if s % NT == NT - 1:
                        act.wait_ge(pv_done, STEPS * g + s + 1 + SLOTS)
                        nc.scalar.activation(acc_sb[:, s // NT, :], acc_ps[:, :], ACT.Copy).then_inc(acc_copied, 1)

            exps(0, 1, range(G))
            with act.Fori(0, NG // 2 - 1) as pair:
                group(pair * 2, 3)
                group(pair * 2 + 1, 3)
            group(NG - 2, 2)
            group(NG - 1, 1)

        @block.vector
        def _(dve):
            dve.sem_inc(normed, 1)
            dve.sem_inc(acc_copied, 1)
            for i in range(2):
                nc.vector.memset(v_grp[i][:, :, :], 0.0)
            nc.vector.memset(neg_max[:, :, :], 0.0)
            dve.drain()
            for i in range(2):
                nc.vector.memset(v_grp[i][:, :, HD:HD + 1], 1.0).then_inc(ones_done, 1)

            def moments(b, before):
                dve.wait_ge(x_in[b], 16)
                for n in range(b * NT, (b + 1) * NT):
                    nc.vector.bn_stats(stats[:, n, :], y_all[:, n, :]).then_inc(stat, 1)
                dve.wait_ge(stat, before + NT)
                for n in range(b * NT, (b + 1) * NT):
                    nc.vector.bn_aggr(mv[:, n, :], stats[:, n, :]).then_inc(stat, 1)

            def add_eps(tiles, before):
                dve.wait_ge(stat, before)
                nc.vector.tensor_scalar(ve[:, tiles], mv[:, tiles, 1], EPS, None, ALU.add).then_inc(stat, 1)

            def root(tiles, i):
                n = 5 * i
                dve.wait_ge(sd_done, i + 1)
                nc.vector.reciprocal(rc[:, tiles], sd[:, tiles]).then_inc(newton, 1)
                dve.wait_ge(newton, n + 1)
                nc.vector.tensor_tensor(nw[:, tiles], ve[:, tiles], rc[:, tiles], ALU.mult).then_inc(newton, 1)
                dve.wait_ge(newton, n + 2)
                nc.vector.tensor_tensor(nw[:, tiles], nw[:, tiles], rc[:, tiles], ALU.mult).then_inc(newton, 1)
                dve.wait_ge(newton, n + 3)
                nc.vector.tensor_scalar(nw[:, tiles], nw[:, tiles], -0.5, 1.5, ALU.mult, ALU.add).then_inc(newton, 1)
                dve.wait_ge(newton, n + 4)
                nc.vector.tensor_tensor(rstd[:, tiles], nw[:, tiles], rc[:, tiles], ALU.mult).then_inc(newton, 1)
                dve.wait_ge(newton, n + 5)
                nc.vector.scalar_tensor_tensor(shift[:, tiles], mv[:, tiles, 0], -1.0, rstd[:, tiles], ALU.mult,
                                               ALU.mult).then_inc(rstd_done, 1)

            def rotate(p, n):
                s, cols = PIECES[p]
                col = (B_S0, B_S1)[s]
                dve.wait_ge(proj_ps, 2 * p + n + 1)
                nc.vector.scalar_tensor_tensor((t1, t2)[n][:, s, cols],
                                               s_ps[:, n, :, :].rearrange("p a c -> p (a c)")[:, cols],
                                               bias_sb[:, col + n:col + n + 1], rope[:, n, cols], ALU.add,
                                               ALU.mult).then_inc(rope_mul, 1)

            moments(0, 0)
            add_eps(slice(0, NT), 2 * NT)
            root(slice(0, NT), 0)
            dve.wait_ge(rstd_done, 1)
            normalise(dve, nc.vector, 0, xn_done, halves=2)
            moments(1, 2 * NT + 1)
            dve.wait_ge(const_in, 48)
            for p in range(2):
                rotate(p, 0)
                rotate(p, 1)
                rotate_sum(dve, nc.vector, p)
            residue(dve, nc.vector, 0)
            residue(dve, nc.vector, 1)
            low_part(dve, nc.vector, 0)
            low_part(dve, nc.vector, 1)
            for b in range(2, B):
                moments(b, 2 * b * NT + 1)
            add_eps(slice(NT, NTT), 2 * NTT + 1)
            root(slice(NT, NTT), 1)
            dve.wait_ge(rstd_done, 2)
            normalise(dve, nc.vector, 1, xn_done, halves=2)
            nc.vector.tensor_copy(ident16[:, :], ident[:, :]).then_inc(id_done, 1)
            dve.wait_ge(ffn_in, 16)
            nc.vector.tensor_scalar(w_ffn[:, :], wi_sb[:, :], DEQUANT, None, ALU.mult).then_inc(w_done, 1)

            def reduce_max(g, a, ps):
                dve.wait_ge(a_ready, AU * g + a + 1)
                h, a = a % AU // HU, a % HU
                nc.vector.tensor_reduce(out=mx[:, h, a // 2, a % 2:a % 2 + 1], in_=ps, op=ALU.max,
                                        axis=AX.X).then_inc(max_done, 1)

            def split_neg(g, h, step):
                n = NEG * (NH * g + h)
                if step == 0:
                    dve.wait_ge(max_done, HU * (NH * g + h + 1))
                    made = nc.vector.tensor_tensor(row_max[:, :], mx[:, h, :, 0], mx[:, h, :, 1], ALU.max)
                else:
                    dve.wait_ge(neg_step, n + step)
                if step == 1:
                    made = nc.vector.tensor_scalar(neg_max[:, 0, :], row_max[:, :], -1.0, None, ALU.mult)
                elif step == 2:
                    made = nc.vector.scalar_tensor_tensor(rest[:, :], row_max[:, :], -1.0, neg_max[:, 0, :], ALU.mult,
                                                          ALU.subtract)
                elif step == 3:
                    made = nc.vector.tensor_copy(neg_max[:, 1, :], rest[:, :])
                elif step == 4:
                    made = nc.vector.tensor_tensor(neg_max[:, 2, :], rest[:, :], neg_max[:, 1, :], ALU.subtract)
                made.then_inc(neg_step, 1)

            def maximum(g, a, ps, last_unit=False):
                reduce_max(g, a, ps)
                done, step = divmod(a + 1, HU)
                if done and step < NEG:
                    half = done - 1
                    for i in range(step, NEG if last_unit else step + 1):
                        split_neg(g + half // NH, half % NH, i)

            for a in range(LEAD):
                maximum(0, a, first_bank(first_slot(a)))
                if a in DVE_S1:
                    rotate(2, DVE_S1.index(a))
            dve.wait_ge(bo_added, B)

            def hidden(g, c, ps):
                dve.wait_ge(tanh_done, FC * g + c + 1)
                nc.vector.scalar_tensor_tensor(gated[:, c, :], th[:, c, :], 1.0, ps[:, 0:CH], ALU.add,
                                               ALU.mult).then_inc(gated_done, 1)
                dve.wait_ge(gated_done, FC * g + c + 1)
                nc.vector.scalar_tensor_tensor(hid[:, c, :], gated[:, c, :], 0.5, ps[:, CH:2 * CH],
                                               ALU.mult, ALU.mult).then_inc(hid_done, 1)

            def add_ffn(g, ps):
                dve.wait_ge(ffn_down, g + 1)
                chunk = y_all[:, bass.ds(g * CT, CT), :]
                nc.vector.tensor_tensor(chunk, chunk, ps[:, 0:CT * D].rearrange("p (t d) -> p t d", t=CT),
                                        ALU.add).then_inc(y_done, 1)

            def normalise_context(g, h, ps):
                ps = ps.rearrange("p (t j c) -> p t j c", t=HT, j=G)
                dve.wait_ge(ctx_ps, NH * g + h + 1)
                nc.vector.reciprocal(rec[:, h, :, :], ps[:, :, :, HD]).then_inc(rec_done, 1)
                dve.wait_ge(rec_done, NH * g + h + 1)
                nc.vector.tensor_tensor(context_half(g, h), ps[:, :, :, 0:HD],
                                        rec[:, h, :, :].unsqueeze(3).to_broadcast([P, HT, G, HD]),
                                        ALU.mult).then_inc(normed, 1)

            def copy_ctx_T(u, ps):
                dve.wait_ge(ctx_T_ps, u + 1)
                nc.vector.tensor_copy(ctx_T[:, (u % 2) * W:(u % 2 + 1) * W], ps).then_inc(ctx_T_done, 1)

            def add_attention(u, ps):
                dve.wait_ge(o_ps, u + 1)
                piece = y_all[:, u * HT:(u + 1) * HT, :]
                nc.vector.tensor_tensor(piece, piece, ps.rearrange("p (t d) -> p t d", d=D),
                                        ALU.add).then_inc(o_done, 1)

            def job(g, slot, kind, n):
                ps = bank(slot)
                if kind == UP:
                    hidden(g, n, ps)
                elif kind == DOWN:
                    add_ffn(g, ps)
                elif kind == CTX:
                    normalise_context(g, n, ps)
                elif kind == STAGE:
                    copy_ctx_T(n, ps)
                elif kind == PROJ:
                    add_attention(n, ps)

            def group(g, order):
                for slot, (kind, n) in enumerate(order):
                    if kind == MAX:
                        maximum(g, n, bank(slot), last_unit=order is LAST_ORDER and n == AU - 1)
                    else:
                        job(g, slot, kind, n)

            for i in range(PER):
                maximum(0, LEAD + i, bank(i - PER))
            with dve.Fori(0, NG // 2 - 1) as pair:
                group(pair * 2, ORDER)
                group(pair * 2 + 1, ORDER)
            group(NG - 2, ORDER)
            group(NG - 1, LAST_ORDER)

        @block.tensor
        def _(pe):
            pe.sem_inc(pv_done, SLOTS)
            pe.wait_ge(w_in, 32)

            def transpose_xn(b, h):
                if b < 2:
                    pe.wait_ge(xn_done, 2 * b + h + 1)
                else:
                    pe.wait_ge(xn_done_pool, b - 1)
                if b == 1 and h == 0:
                    pe.wait_ge(rope_mul, 1)
                if b >= 1:
                    pe.wait_ge(xnt_done, 2 * b + h - 1)
                for t in range(HT):
                    last = nc.tensor.transpose((s_ps[:, 0, 0, :], acc_ps[:, :])[h][:, t * P:(t + 1) * P], xn[:, b, h * HT + t, :],
                                               ident[:, :])
                last.then_inc(xnt_ps, 1)

            def project(c, b, n, h):
                return nc.tensor.matmul(s_ps[:, n, h, :], wf_sb[:, c + n * D:c + (n + 1) * D],
                                        xn_T[:, b * T + h * W:b * T + (h + 1) * W], start=True, stop=True)

            def project_tiles(n, h, columns):
                for b, c in enumerate(columns):
                    last = nc.tensor.matmul(s_ps[32 * b:32 * b + 32, n, h, :], wf_sb[:, c:c + 32],
                                            xn_T[:, b * T + h * W:b * T + (h + 1) * W], start=True, stop=True)
                return last

            for h in range(2):
                transpose_xn(0, h)
            for h in range(2):
                pe.wait_ge(xnt_done, h + 1)
                for n in range(2):
                    project(C_S0, 0, n, h).then_inc(proj_ps, 1)
            for h in range(2):
                transpose_xn(1, h)

            def max_unit(par, a, ps):
                h, r = a // HU, a % HU
                j, t, k = r // (HT * 2), h * HT + r // 2 % HT, r % 2
                nc.tensor.matmul(ps, qa[par][0:MAX_ROW, j, t * P:(t + 1) * P],
                                 ka[par][0:MAX_ROW, k * W:(k + 1) * W], start=True, stop=True).then_inc(a_ready, 1)

            def transpose_neg(g, h, ps):
                pe.wait_ge(neg_step, NEG * (NH * g + h + 1))
                nc.tensor.transpose(ps.bitcast(BF16)[0:2 * PARTS * G * HT, 0:P], neg_max[:, :, :], ident16[:, :])\
                    .then_inc(neg_T_ps, 1)

            def scores(g, par, s, j):
                kt, h = s % NT, s // NT
                u = G * s + j
                if kt == 0 and j == 0:
                    pe.wait_ge(neg_loaded, (NH * g + h + 1) * 16 * PARTS)
                pe.wait_ge(exp_done, SG * g + score_before(u) + 1 + G)
                nc.tensor.matmul(banks[:, score_bank(u), :], kc[par][:, kt * P:(kt + 1) * P],
                                 qc[par][:, h, j, :], start=True, stop=True).then_inc(scores_ready, 1)

            pe.wait_ge(qa_loaded[0], DMAS)
            for a in range(LEAD):
                if a >= FIRST_RING:
                    pe.wait_ge(max_done, a + 1 - FIRST_RING + (NEG_BEHIND < a <= NEG_BEHIND + FIRST_RING))
                if a == NEG_BEHIND + FIRST_RING:
                    pe.wait_ge(neg_T_done, 1)
                max_unit(0, a, first_bank(first_slot(a)))
                if a in PE_XN:
                    transpose_xn(2 + PE_XN.index(a) // 2, PE_XN.index(a) % 2)
                if a in PE_S1:
                    n, h = divmod(PE_S1.index(a), 2)
                    if h == 0:
                        pe.wait_ge(xnt_done, 2 * B)
                        pe.wait_ge(rope_mul, 3 + n)
                    last = project_tiles(n, h, [C_Q + n * D + Q_ROWS] + [C_K + n * 32] * (B - 1))
                    if h == 1:
                        last.then_inc(proj_ps, 1)
                if a in PE_V:
                    h = PE_V.index(a)
                    if h == 0:
                        pe.wait_ge(rope_mul, 5)
                    last = project_tiles(0, h, [C_V] * B)
                    if h == 1:
                        last.then_inc(vt_ps, 1)
                if a in PE_VT:
                    h = PE_VT.index(a)
                    if h == 0:
                        pe.wait_ge(vt_done, 1)
                        pe.wait_ge(rope_mul, 6)
                    for t in range(h * HT, (h + 1) * HT):
                        last = nc.tensor.transpose(s_ps[:, 1, t // 4, t % 4 * P:(t % 4 + 1) * P],
                                                   v_T[:, t * P:(t + 1) * P], ident[:, :])
                    if h == 1:
                        last.then_inc(v_ps, 1)
                if a in PE_Q:
                    b, n, h = 1 + PE_Q.index(a) // 4, PE_Q.index(a) // 2 % 2, PE_Q.index(a) % 2
                    if h == 0:
                        if b > 1:
                            pe.wait_ge(raw_done, 2 * (b - 2) + n + 1)
                        elif n == 1:
                            pe.wait_ge(v_done, 1)
                    last = project(C_Q, b, n, h)
                    if h == 1:
                        last.then_inc(q_ps, 1)
                if a == NEG_BEHIND:
                    pe.wait_ge(id_done, 1)
                    pe.wait_ge(max_done, a - 1)
                    transpose_neg(0, 0, first_bank(NEG_BEHIND + 1))
            pe.wait_ge(raw_done, 2 * (B - 1))
            pe.wait_ge(w_done, 1)
            pe.wait_ge(qc_loaded[0], DMAS_C)
            for j in range(G):
                scores(0, 0, 0, j)

            def weigh(g, par, s):
                kt, h = s % NT, s // NT
                if s == 0:
                    pe.wait_ge(v_grp_done, g + 1)
                if kt == 0:
                    pe.wait_ge(acc_copied, NH * g + h + 1)
                pe.wait_ge(exp_done, SG * g + G * (s + 1) + G)
                for j in range(G):
                    last = nc.tensor.matmul(acc_ps[VC * j:VC * (j + 1), :], v_grp[par][:, kt, :],
                                            probs[:, s % SLOTS, j, :], start=(kt == 0), stop=(kt == NT - 1))
                last.then_inc(pv_done, 1)

            def ffn_gate_up(g, c, ps):
                for n in range(2):
                    last = nc.tensor.matmul(ps[:, n * CH:(n + 1) * CH],
                                            w_ffn[:, n * HID + c * P:n * HID + (c + 1) * P],
                                            xn_T[:, bass.ds(g * CH, CH)], start=True, stop=True)
                last.then_inc(ffn_up, 1)

            def ffn_down_proj(g, ps):
                pe.wait_ge(hid_done, FC * (g + 1))
                for t in range(CT):
                    for c in range(FC):
                        last = nc.tensor.matmul(ps[:, t * D:(t + 1) * D], hid[:, c, t * P:(t + 1) * P],
                                                w_ffn[:, 2 * HID + c * D:2 * HID + (c + 1) * D],
                                                start=(c == 0), stop=(c == FC - 1))
                last.then_inc(ffn_down, 1)

            def transpose_context(g, h, ps):
                pe.wait_ge(acc_copied, NH * g + h + 2)
                for t in range(HT):
                    last = nc.tensor.transpose(ps[:, t * P:(t + 1) * P], acc_sb[:, h, t * P:(t + 1) * P],
                                               ident[:, :])
                last.then_inc(ctx_ps, 1)

            def transpose_stage(u, ps):
                pe.wait_ge(staged, u + 1)
                for t in range(HT):
                    last = nc.tensor.transpose(ps[:, t * P:(t + 1) * P], stage[:, u // 2, (u % 2) * HT + t, :],
                                               ident[:, :])
                last.then_inc(ctx_T_ps, 1)

            def project_out(u, ps):
                pe.wait_ge(ctx_T_done, u + 1)
                for t in range(HT):
                    c = (u % 2) * W + t * P
                    last = nc.tensor.matmul(ps[:, t * D:(t + 1) * D], ctx_T[:, c:c + P], wf_sb[:, C_O:C_O + D],
                                            start=True, stop=True)
                last.then_inc(o_ps, 1)

            def bank_left(g, kind, n, back=0):
                if kind == MAX:
                    pe.wait_ge(max_done, AU * g + n + 1 - AU * back)
                elif kind == UP:
                    pe.wait_ge(hid_done, FC * g + n + 1 - FC * back)
                elif kind == DOWN:
                    pe.wait_ge(y_done, g + 1 - back)
                elif kind == NEG_T:
                    pe.wait_ge(neg_T_done, NH * g + NH * (1 - n) + n + 1 - NH * back)
                elif kind == CTX:
                    pe.wait_ge(normed, NH * g + n + 2 - NH * back)
                elif kind == STAGE:
                    pe.wait_ge(ctx_T_done, n + 1)
                elif kind == PROJ:
                    pe.wait_ge(o_done, n + 1)

            def take(g, par, slot, order):
                if slot >= RING:
                    bank_left(g, *order[slot - RING])
                else:
                    bank_left(g, *ORDER[slot - RING], back=1)
                kind, n = order[slot]
                ps = bank(slot)
                if kind == MAX:
                    max_unit(par if n < AU else 1 - par, n % AU, ps)
                elif kind == UP:
                    ffn_gate_up(g, n, ps)
                elif kind == DOWN:
                    ffn_down_proj(g, ps)
                elif kind == NEG_T:
                    transpose_neg(g + 1 - n, n, ps)
                elif kind == CTX:
                    transpose_context(g, n, ps)
                elif kind == STAGE:
                    transpose_stage(n, ps)
                elif kind == PROJ:
                    project_out(n, ps)

            def next_scores(g, pair, par, s, j):
                s += 1
                if s == STEPS and j == 0:
                    if par == 0:
                        pe.wait_ge(qc_loaded[1], (pair + 1) * DMAS_C)
                    else:
                        pe.wait_ge(qc_loaded[0], (pair + 2) * DMAS_C)
                scores(g + s // STEPS, par if s < STEPS else 1 - par, s % STEPS, j)

            def group(g, pair, par, left):
                order = LAST_ORDER if left == 1 else ORDER
                slot = 0
                for s in range(1, STEPS + (left > 1)):
                    if PER * s + LEAD == AU and left > 1:
                        if par == 0:
                            pe.wait_ge(qa_loaded[1], (pair + 1) * DMAS)
                        else:
                            pe.wait_ge(qa_loaded[0], (pair + 2) * DMAS)
                    if PER * (s + 1) + LEAD == AU and left > 2:
                        pe.wait_ge(q_stored, pair + 1)
                    todo = step_order(s, left == 1)
                    units = [o for o in todo if o[0] == MAX]
                    more = s + 1 < STEPS or left > 1
                    for j in range(G - 1):
                        if units:
                            take(g, par, slot, order)
                            slot += 1
                        if more:
                            next_scores(g, pair, par, s, j)
                    for _ in range(len(todo) - len(units)):
                        take(g, par, slot, order)
                        slot += 1
                    weigh(g + s // STEPS, par if s < STEPS else 1 - par, s % STEPS)
                    if units:
                        take(g, par, slot, order)
                        slot += 1
                    if more:
                        next_scores(g, pair, par, s, G - 1)
                for slot in range(slot, len(order)):
                    take(g, par, slot, order)

            for i in range(PER):
                if i > 0:
                    pe.wait_ge(max_done, LEAD + i - FIRST_RING)
                if i == PER - 1:
                    weigh(0, 0, 0)
                max_unit(0, LEAD + i, bank(i - PER))
                scores(0, 0, 1, i)

            with pe.Fori(0, NG // 2 - 1) as pair:
                group(pair * 2, pair, 0, 3)
                group(pair * 2 + 1, pair, 1, 3)
            group(NG - 2, NG // 2 - 1, 0, 2)
            group(NG - 1, NG // 2 - 1, 1, 1)


_INS = ["x", "wf", "wi", "biases", "bo", "tables", "identity"]


def kernel(**inputs):
    import numpy as np
    import concourse.bacc as bacc
    from concourse.bass_utils import run_bass_kernel_spmd

    p = "L0_attn_"
    a = {k: np.asarray(v) for k, v in inputs.items()}
    half = [1, 3, 5, 7, 0, 2, 4, 6]
    q_rows = [h * HD + r for h in range(H) for r in half]
    k_rows = [h * HD + r for h in range(KV) for r in half]
    wq, wk, wv, wo = (a[p + n] for n in ("Wq", "Wk", "Wv", "Wo"))
    bq, bk, bv = (a[p + n] for n in ("bq", "bk", "bv"))
    first, first_rotated = (np.concatenate([q[:Q_ROWS], k]) for q, k in ((wq, wk), (wq[q_rows], wk[k_rows])))
    wf = np.concatenate([first.T, first_rotated.T, wq.T, wq[q_rows].T, wk.T, wk[k_rows].T, wv.T, wo.T], axis=1)
    down = a["L0_ffn_w_down"].T.reshape(FC, P, D).transpose(1, 0, 2).reshape(P, FC * D)
    wi = np.concatenate([a["L0_ffn_w_gate"].T, a["L0_ffn_w_up"].T, down], axis=1)
    b_q = [bq, bq[q_rows]]
    b_k = [bk, bk[k_rows]]
    biases = np.stack([np.concatenate([q[:Q_ROWS], k]) for q, k in zip(b_q, b_k)]
                      + [np.concatenate([q[Q_ROWS:]] + [k] * (B - 1)) for q, k in zip(b_q, b_k)]
                      + b_q + [np.tile(bv, B)], axis=1)
    freq = (np.float32(1.0) / np.float32(10000.0) ** (np.arange(0, HD, 2, dtype=np.float32) / np.float32(HD)))
    angle = np.arange(T, dtype=np.float32)[None, :] * freq.astype(np.float32)[:, None]
    cos = np.tile(np.cos(angle), (P // len(freq), 1))
    sin = np.tile(np.concatenate([-np.sin(angle), np.sin(angle)], axis=0), (P // HD, 1))
    tables = np.stack([cos, sin], axis=1).astype(np.float32)

    arrays = {
        "x": a[p + "hidden_states"], "wf": wf, "wi": wi, "biases": biases, "bo": a[p + "bo"], "tables": tables,
        "identity": np.eye(P, dtype=np.float32),
    }
    nc = bacc.Bacc("TRN2", target_bir_lowering=False, num_devices=1)
    arrays = {f"in_{n}": np.ascontiguousarray(arrays[n]) for n in _INS}
    aps = [nc.dram_tensor(n, v.shape, mybir.dt.from_np(v.dtype), kind="ExternalInput").ap() for n, v in arrays.items()]
    out = nc.dram_tensor("out_0", (B, T, D), F32, kind="ExternalOutput").ap()
    attention_swiglu(nc, *aps, out)
    r = run_bass_kernel_spmd(nc, [arrays], core_ids=[0])
    return r.results[0]["out_0"]
```

```python
from contextlib import ExitStack

import concourse.bass as bass
from concourse import mybir

F32 = mybir.dt.float32
BF16 = mybir.dt.bfloat16
I32 = mybir.dt.int32
ALU = mybir.AluOpType
ACT = mybir.ActivationFunctionType
AX = mybir.AxisListType

B, T, D = 4, 1024, 128
H, G = 16, 4
HD = D // H
KV = H // G
HID = 384
P = 128
W = 512
NT = T // P
NTT = B * NT
NG = B * KV
PARTS = 3
ROWS = PARTS * HD
MAX_ROW = 96
NH = T // W
HT = NT // NH
STEPS = NH * NT
SLOTS = 2
HU = G * HT * 2
AU = NH * HU
PER = AU // STEPS
LEAD = 48
S_BANKS = 3
RING = 4
FIRST_RING = 3
SG = G * STEPS
CH = T * B // NG
CT = CH // P
FC = HID // P
VC = 32
SCALE = HD ** -0.5
DEQUANT = 1.0 / 127.0
EPS = 1e-5
C_S0, C_Q, C_K = 0, 2 * D, 4 * D
C_V = C_K + 2 * 32
C_O = C_V + 32
C_ALL = C_O + D
B_S0, B_S1, B_Q, B_V = 0, 2, 4, 6
Q_ROWS = P - HD * KV
PROJECTED = (1, 0, 2, 3)
assert len(PROJECTED) == B
PE_XN, PE_S1, PE_V, PE_VT, PE_Q = (3, 5, 7, 9), (11, 13, 15, 17), (19, 21), (23, 24), tuple(range(26, 42, 2))
NEG_BEHIND = HU + 5
MAX, UP, DOWN, NEG_T, CTX, STAGE, PROJ = "max", "up", "down", "neg_T", "ctx", "stage", "proj"
JOB_AT = {1: (UP, 0), 3: (UP, 1), 5: (NEG_T, 1), 7: (UP, 2), 8: (CTX, 0), 10: (DOWN, 0), 13: (NEG_T, 0), 16: (CTX, 1)}
OUT_AT = (4, 5, 6, 7, 8, 9, 12)
OUTS = 2 * B


def step_order(s, last_group):
    if last_group:
        units = [(MAX, PER * s + LEAD + i) for i in range(PER) if PER * s + LEAD < AU]
        jobs = [JOB_AT[s]] if s in JOB_AT and JOB_AT[s] != (NEG_T, 0) else []
        jobs += [(PROJ, OUT_AT.index(s - 1))] if s - 1 in OUT_AT else []
        jobs += [(STAGE, OUT_AT.index(s))] if s in OUT_AT else []
    else:
        units = [(MAX, PER * s + LEAD + i) for i in range(PER)]
        jobs = [JOB_AT[s]] if s in JOB_AT else []
    return units[:3] + jobs + units[3:]


ORDER = [o for s in range(1, STEPS + 1) for o in step_order(s, False)]
LAST_ORDER = [o for s in range(1, STEPS) for o in step_order(s, True)]
LAST_ORDER += [JOB_AT[STEPS], (STAGE, OUTS - 1), (PROJ, OUTS - 1)]
assert len(ORDER) % RING == 0


def score_bank(u):
    return u % S_BANKS if u < SG - 1 else 1


def score_before(u):
    return max(v for v in range(-SG, u) if score_bank(v % SG) == score_bank(u))


def attention_swiglu(nc, x, wf, wi, biases, bo, tables, identity, out):
    q_parts = nc.dram_tensor("q_parts", (NG, G, HD, PARTS, T), BF16, kind="Internal").ap()
    k_parts = nc.dram_tensor("k_parts", (NG, HD, PARTS, T), BF16, kind="Internal").ap()

    with ExitStack() as ctx:
        def sb(name, shape, dt=F32):
            return ctx.enter_context(nc.sbuf_tensor(name, shape, dt))

        def sem(name):
            return ctx.enter_context(nc.semaphore(name))

        def sems(name, n=2):
            return [sem(f"{name}{i}") for i in range(n)]

        ident = sb("ident", [P, P])
        ident16 = sb("ident16", [P, P], BF16)
        wf_sb = sb("wf_sb", [P, C_ALL])
        wi_sb = sb("wi_sb", [P, 3 * HID], I32)
        w_ffn = sb("w_ffn", [P, 3 * HID])
        bias_sb = sb("bias_sb", [P, B_V + 1])
        bo_sb = sb("bo_sb", [P, D])
        rope = sb("rope", [P, 2, T])
        y_all = sb("y_all", [P, NTT, D])
        xn_T = sb("xn_T", [P, B * T])
        ctx_all = sb("ctx_all", [P, NT, NG, G * HD])
        v_all = sb("v_all", [P, NT, NG, HD])
        v_grp = [sb(f"v_grp{i}", [P, NT, VC]) for i in range(2)]
        qa = [sb(f"qa{i}", [P, G, T], BF16) for i in range(2)]
        ka = [sb(f"ka{i}", [P, T], BF16) for i in range(2)]
        qc = [sb(f"qc{i}", [P, NH, G, W], BF16) for i in range(2)]
        kc = [sb(f"kc{i}", [P, T], BF16) for i in range(2)]
        probs = sb("probs", [P, SLOTS, G, W])
        acc_sb = sb("acc_sb", [P, NH, W])
        mx = sb("mx", [P, NH, G * HT, 2])
        row_max = sb("row_max", [P, G * HT])
        rest = sb("rest", [P, G * HT])
        neg_max = sb("neg_max", [P, 2 * PARTS, G * HT], BF16)
        neg_max_T = sb("neg_max_T", [PARTS * G * HT, P], BF16)
        th = sb("th", [P, FC, CH])
        gated = sb("gated", [P, FC, CH])
        hid = sb("hid", [P, FC, CH])
        rec = sb("rec", [P, NH, HT, G])
        stats = sb("stats", [P, NTT, 6])
        mv = sb("mv", [P, NTT, 2])
        ve = sb("ve", [P, NTT])
        sd = sb("sd", [P, NTT])
        rc = sb("rc", [P, NTT])
        nw = sb("nw", [P, NTT])
        rstd = sb("rstd", [P, NTT])
        shift = sb("shift", [P, NTT])
        xn = sb("xn", [P, B, NT, D])
        t1, t2 = (probs[:, 0, 2 * i:2 * i + 2, :].rearrange("p a c -> p (a c)") for i in range(2))
        rot, res = (ctx_all[:, i * NT // 2:(i + 1) * NT // 2, :, :].rearrange("p t g c -> p (t g c)")[:, 0:T]
                    for i in range(2))
        part = sb("part", [P, 2, PARTS, T], BF16)
        v_T = sb("v_T", [P, T])
        raw = [probs[:, 1, :, :].rearrange("p (n a) c -> p n (a c)", n=2),
               xn[:, 0:2, :, :].rearrange("p n t d -> p n (t d)"),
               xn[:, 2:4, :, :].rearrange("p n t d -> p n (t d)"), sb("raw", [P, 2, T])[:, :, :]]
        ctx_T = v_T

        acc_ps = ctx.enter_context(nc.psum_tensor("acc_ps", [P, W], F32))
        banks = ctx.enter_context(nc.psum_tensor("banks", [P, S_BANKS + RING, W], F32))
        s_ps = banks[:, 0:4, :].rearrange("p (n h) w -> p n h w", n=2)

        xnt_banks = (banks[:, 0, :], acc_ps[:, :])

        def bank(slot):
            return banks[:, S_BANKS + (slot + PER) % RING, :]

        def first_bank(slot):
            return banks[:, 4 + (slot - LEAD - 1) % FIRST_RING, :]

        def first_slot(a):
            return a + (a > NEG_BEHIND)

        x_in = sems("x_in", B)
        w_in = sem("w_in")
        const_in = sem("const_in")
        ffn_in = sem("ffn_in")
        zeroed = sem("zeroed")
        ones_done = sem("ones_done")
        stat = sem("stat")
        sd_done = sem("sd_done")
        newton = sem("newton")
        rstd_done = sem("rstd_done")
        xn_done = sem("xn_done")
        xn_done_act = sem("xn_done_act")
        xn_done_pool = sem("xn_done_pool")
        xnt_ps = sem("xnt_ps")
        xnt_done = sem("xnt_done")
        proj_ps = sem("proj_ps")
        rope_mul = sem("rope_mul")
        rope_sum = sem("rope_sum")
        part_hi = sem("part_hi")
        part_res = sem("part_res")
        part_mid = sem("part_mid")
        part_lo = sem("part_lo")
        q_ps = sem("q_ps")
        raw_done = sem("raw_done")
        q_step = sem("q_step")
        q_dma = sem("q_dma")
        q_stored = sem("q_stored")
        k_stored = sems("k_stored")
        q_stored_too = sems("q_stored_too")
        vt_ps = sem("vt_ps")
        vt_done = sem("vt_done")
        v_ps = sem("v_ps")
        v_done = sem("v_done")
        w_done = sem("w_done")
        id_done = sem("id_done")
        bo_added = sem("bo_added")
        qa_loaded = sems("qa_loaded")
        qc_loaded = sems("qc_loaded")
        v_grp_done = sem("v_grp_done")
        a_ready = sem("a_ready")
        max_done = sem("max_done")
        neg_step = sem("neg_step")
        neg_T_ps = sem("neg_T_ps")
        neg_T_done = sem("neg_T_done")
        neg_loaded = sem("neg_loaded")
        scores_ready = sem("scores_ready")
        exp_done = sem("exp_done")
        pv_done = sem("pv_done")
        acc_copied = sem("acc_copied")
        ffn_up = sem("ffn_up")
        tanh_done = sem("tanh_done")
        gated_done = sem("gated_done")
        hid_done = sem("hid_done")
        ffn_down = sem("ffn_down")
        y_done = sem("y_done")
        ctx_ps = sem("ctx_ps")
        rec_done = sem("rec_done")
        normed = sem("normed")
        ctx_T_ps = sem("ctx_T_ps")
        ctx_T_done = sem("ctx_T_done")
        o_ps = sem("o_ps")
        o_done = sem("o_done")
        out_stored = sem("out_stored")

        NEG = 5
        Q_STEPS = 7
        DMAS = 16 * 2 * PARTS
        DMAS_C = 16 * (NH + 1) * PARTS
        block = ctx.enter_context(nc.Block())

        def context_half(g, h):
            return ctx_all[:, h * HT:(h + 1) * HT, g, :].rearrange("p t (j d) -> p t j d", j=G)

        def normalise(eng, ops, b, done, halves=1):
            for t in range(NT):
                n = b * NT + t
                last = ops.tensor_scalar(xn[:, b, t, :], y_all[:, n, :], rstd[:, n:n + 1], shift[:, n:n + 1],
                                         ALU.mult, ALU.add)
                if (t + 1) % (NT // halves) == 0:
                    last.then_inc(done, 1)

        HALF = [slice(h * W, (h + 1) * W) for h in range(2)]

        @block.sync
        def _(sp):
            for b in range(B):
                sp.dma_start(y_all[:, b * NT:(b + 1) * NT, :],
                             x[b].rearrange("(t p) d -> p t d", p=P)).then_inc(x_in[b], 16)

            def load_k(g, k_buf, loaded):
                for n in range(PARTS):
                    sp.dma_start(k_buf[n * ROWS:(n + 1) * ROWS, :],
                                 k_parts[g, :, n, :].unsqueeze(1).to_broadcast([HD, PARTS, T])).then_inc(loaded, 16)

            def load_q(g, q_buf, loaded):
                q_rows = q_parts[g].rearrange("j d n t -> (d n) j t")
                for c in range(PARTS):
                    if q_buf in qa:
                        sp.dma_start(q_buf[c * ROWS:(c + 1) * ROWS, :, :], q_rows).then_inc(loaded, 16)
                    else:
                        for h in range(NH):
                            sp.dma_start(q_buf[c * ROWS:(c + 1) * ROWS, h, :, :],
                                         q_rows[:, :, h * W:(h + 1) * W]).then_inc(loaded, 16)

            def load_parts(g, q_buf, k_buf, loaded):
                load_k(g, k_buf, loaded)
                load_q(g, q_buf, loaded)

            def load_neg(g, h, par):
                sp.wait_ge(neg_T_done, NH * g + h + 1)
                rows = qc[par][MAX_ROW:MAX_ROW + PARTS, h, :, :].rearrange("n j c -> n (j c)")
                sp.dma_start(rows, neg_max_T[:, :]).then_inc(neg_loaded, 16)

            sp.wait_ge(part_lo, 2)
            sp.dma_start(k_parts[0:KV].rearrange("g d n t -> (g d) n t"), part[Q_ROWS:P, 0, :, :])\
                .then_inc(k_stored[0], 16)
            sp.dma_start(q_parts[0:KV - 1].rearrange("g j d n t -> (g j d) n t"), part[0:Q_ROWS, 0, :, :])\
                .then_inc(q_stored_too[0], 16)
            sp.wait_ge(zeroed, 10)
            sp.wait_ge(k_stored[0], 16)
            load_k(0, ka[0], qa_loaded[0])
            sp.wait_ge(q_stored_too[0], 16)
            load_q(0, qa[0], qa_loaded[0])
            load_parts(0, qc[0], kc[0], qc_loaded[0])
            load_neg(0, 0, 0)
            sp.wait_ge(q_step, Q_STEPS)
            sp.dma_start(k_parts[KV:NG].rearrange("g d n t -> (g d) n t"), part[P - Q_ROWS:P, 1, :, :])\
                .then_inc(k_stored[1], 16)
            sp.dma_start(q_parts[KV - 1].rearrange("j d n t -> (j d) n t"), part[0:P - Q_ROWS, 1, :, :])\
                .then_inc(q_stored_too[1], 16)
            sp.wait_ge(k_stored[1], 16)
            sp.wait_ge(q_stored_too[1], 16)
            load_parts(1, qa[1], ka[1], qa_loaded[1])

            def group(g, par, left):
                if left > 1:
                    sp.wait_ge(pv_done, STEPS * g + SLOTS)
                    load_parts(g + 1, qc[1 - par], kc[1 - par], qc_loaded[1 - par])
                load_neg(g, 1, par)
                if left > 2:
                    sp.wait_ge(a_ready, AU * (g + 1))
                    load_parts(g + 2, qa[par], ka[par], qa_loaded[par])
                if left > 1:
                    load_neg(g + 1, 0, 1 - par)

            with sp.Fori(0, NG // 2 - 1) as pair:
                group(pair * 2, 0, 3)
                group(pair * 2 + 1, 1, 3)
            group(NG - 2, 0, 2)
            group(NG - 1, 1, 1)

            for u in range(OUTS):
                sp.wait_ge(o_done, u + 1)
                sp.dma_start(out[u // 2, (u % 2) * W:(u % 2 + 1) * W, :].rearrange("(t p) d -> p t d", p=P),
                             y_all[:, u * HT:(u + 1) * HT, :]).then_inc(out_stored, 16)
            sp.wait_ge(out_stored, 16 * OUTS)

        @block.gpsimd
        def _(pool):
            for i in range(2):
                for t in (qa[i][64:P].rearrange("p j t -> p (j t)"), qc[i][64:P].rearrange("p h j w -> p (h j w)")):
                    nc.gpsimd.memset(t.bitcast(F32), 0.0).then_inc(zeroed, 1)
                for t in (ka[i][:, :], kc[i][:, :]):
                    nc.gpsimd.memset(t[64:P].bitcast(F32), 0.0).then_inc(zeroed, 1)
            pool.wait_ge(zeroed, 8)
            for i in range(2):
                nc.gpsimd.memset(kc[i][MAX_ROW:MAX_ROW + PARTS, :], 1.0).then_inc(zeroed, 1)
            pool.wait_ge(zeroed, 10)
            pool.sem_inc(q_stored, 1)
            for b, n in ((1, 2), (2, 3)):
                pool.wait_ge(rstd_done, n)
                normalise(pool, nc.gpsimd, b, xn_done_pool)

            def split_later(i):
                slot, n = (i + 1) % 2, Q_STEPS * i
                rows, twin = (raw[i][:, k, :] for k in range(2))
                pool.wait_ge(raw_done, 2 * PROJECTED.index(i) + 2)
                nc.gpsimd.tensor_tensor(rows, rows, rope[:, 0, :], ALU.mult).then_inc(q_step, 1)
                nc.gpsimd.tensor_tensor(twin, twin, rope[:, 1, :], ALU.mult).then_inc(q_step, 1)
                pool.wait_ge(q_step, n + 2)
                nc.gpsimd.tensor_tensor(rows, rows, twin, ALU.add).then_inc(q_step, 1)
                if i in (1, 2):
                    pool.wait_ge(k_stored[i - 1], 16)
                    pool.wait_ge(q_stored_too[i - 1], 16)
                pool.wait_ge(q_step, n + 3)
                nc.gpsimd.tensor_copy(part[:, slot, 0, :], rows).then_inc(q_step, 1)
                pool.wait_ge(q_step, n + 4)
                nc.gpsimd.tensor_tensor(twin, rows, part[:, slot, 0, :], ALU.subtract).then_inc(q_step, 1)
                pool.wait_ge(q_step, n + 5)
                nc.gpsimd.tensor_copy(part[:, slot, 1, :], twin).then_inc(q_step, 1)
                pool.wait_ge(q_step, n + 6)
                nc.gpsimd.tensor_tensor(part[:, slot, 2, :], twin, part[:, slot, 1, :],
                                        ALU.subtract).then_inc(q_step, 1)
                pool.wait_ge(q_step, n + 7)

            pool.wait_ge(const_in, 48)
            split_later(0)

            def copy_v(g, par):
                nc.gpsimd.tensor_copy(v_grp[par][:, :, 0:HD], v_all[:, :, g, :]).then_inc(v_grp_done, 1)

            pool.wait_ge(ones_done, 2)
            pool.wait_ge(v_done, 1)
            copy_v(0, 0)
            copy_v(1, 1)
            pool.wait_ge(xn_done, 2)
            pool.wait_ge(xn_done_act, 1)
            for b in range(B):
                nc.gpsimd.tensor_tensor(y_all[:, b * NT:(b + 1) * NT, :], y_all[:, b * NT:(b + 1) * NT, :],
                                        bo_sb[:, :].unsqueeze(1).to_broadcast([P, NT, D]),
                                        ALU.add).then_inc(bo_added, 1)

            for b in range(1, B):
                split_later(b)
                pool.dma_start(q_parts[b * KV:(b + 1) * KV].rearrange("g j d n t -> (g j d) n t"),
                               part[:, (b + 1) % 2, :, :]).then_inc(q_dma, 16)
                pool.wait_ge(q_dma, 16 * b)
                pool.sem_inc(q_stored, 2)

            def group(g, par):
                pool.wait_ge(pv_done, STEPS * (g + 1) + SLOTS)
                copy_v(g + 2, par)

            with pool.Fori(0, NG // 2 - 1) as pair:
                group(pair * 2, 0)
                group(pair * 2 + 1, 1)

        @block.scalar
        def _(act):
            act.dma_start(ident[:, :], identity).then_inc(w_in, 16)
            act.dma_start(wf_sb[:, :], wf).then_inc(w_in, 16)
            act.dma_start(bias_sb[:, :], biases).then_inc(const_in, 16)
            act.dma_start(rope[:, :, :], tables).then_inc(const_in, 16)
            act.dma_start(bo_sb[:, :], bo.partition_broadcast(P)).then_inc(const_in, 16)
            act.dma_start(wi_sb[:, :], wi).then_inc(ffn_in, 16)
            act.sem_inc(exp_done, G)

            def root(tiles, n):
                act.wait_ge(stat, n)
                nc.scalar.activation(sd[:, tiles], ve[:, tiles], ACT.Sqrt).then_inc(sd_done, 1)

            def copy_xn_T(b):
                for h in range(2):
                    act.wait_ge(xnt_ps, 2 * b + h + 1)
                    nc.scalar.activation(xn_T[:, b * T + h * W:b * T + (h + 1) * W], xnt_banks[h],
                                         ACT.Copy).then_inc(xnt_done, 1)

            def split_high(h):
                act.wait_ge(rope_sum, h + 1)
                nc.scalar.activation(part[:, 0, 0, HALF[h]], rot[:, HALF[h]], ACT.Copy).then_inc(part_hi, 1)

            def split_mid(h):
                act.wait_ge(part_res, h + 1)
                nc.scalar.activation(part[:, 0, 1, HALF[h]], res[:, HALF[h]], ACT.Copy).then_inc(part_mid, 1)

            def copy_later(i, n):
                col = (B_Q if i else B_S1) + n
                act.wait_ge(q_ps, 2 * PROJECTED.index(i) + n + 1)
                nc.scalar.activation(raw[i][:, n, :], s_ps[:, n, :, :].rearrange("p a c -> p (a c)"), ACT.Identity,
                                     bias=bias_sb[:, col:col + 1]).then_inc(raw_done, 1)

            def copy_neg(g, h, ps):
                act.wait_ge(neg_T_ps, NH * g + h + 1)
                nc.scalar.activation(neg_max_T[:, :], ps.bitcast(BF16)[0:PARTS * G * HT, 0:P],
                                     ACT.Copy).then_inc(neg_T_done, 1)

            def exps(g, s, heads):
                for j in heads:
                    if j == 0:
                        act.wait_ge(pv_done, STEPS * g + s + 1)
                    act.wait_ge(scores_ready, SG * g + G * s + j + 1)
                    nc.scalar.activation(probs[:, s % SLOTS, j, :], banks[:, score_bank(G * s + j), :], ACT.Exp,
                                         scale=SCALE).then_inc(exp_done, 1)

            root(slice(0, NT), 2 * NT + 1)
            copy_xn_T(0)
            root(slice(NT, 2 * NT), 4 * NT + 2)
            split_high(0)
            split_high(1)
            split_mid(0)
            split_mid(1)
            copy_xn_T(1)
            act.wait_ge(const_in, 48)
            copy_later(1, 0)
            root(slice(2 * NT, NTT), 2 * NTT + 3)
            nc.scalar.preload_act_table(ACT.Exp)
            copy_later(1, 1)
            act.wait_ge(rstd_done, 3)
            for t in range(NT):
                n = (B - 1) * NT + t
                last = nc.scalar.activation(xn[:, B - 1, t, :], y_all[:, n, :], ACT.Identity,
                                            bias=shift[:, n:n + 1], scale=rstd[:, n:n + 1])
            last.then_inc(xn_done_act, 1)
            for b in range(2, B):
                copy_xn_T(b)
            for n in range(2):
                copy_later(0, n)
            act.wait_ge(vt_ps, 1)
            nc.scalar.activation(v_T[:, :], s_ps[:, 0, :, :], ACT.Identity,
                                 bias=bias_sb[:, B_V:B_V + 1]).then_inc(vt_done, 1)
            act.wait_ge(v_ps, 1)
            nc.scalar.activation(v_all[:, :, :, :], s_ps[:, 1, :, :], ACT.Copy).then_inc(v_done, 1)
            for i in PROJECTED[2:]:
                for n in range(2):
                    if (i, n) == (PROJECTED[-1], 1):
                        copy_neg(0, 0, first_bank(NEG_BEHIND + 1))
                    copy_later(i, n)
            act.wait_ge(rope_sum, 2)
            exps(0, 0, range(G))

            def group(g, left):
                slot = 0
                for s in range(1, STEPS + (left > 1)):
                    after = (g + (s + 1) // STEPS, (s + 1) % STEPS)
                    more = s + 1 < STEPS or left > 1
                    if more:
                        exps(*after, range(G - 1))
                    for kind, n in step_order(s, left == 1):
                        if kind == UP:
                            act.wait_ge(ffn_up, FC * g + n + 1)
                            nc.scalar.activation(th[:, n, :], bank(slot)[:, 0:CH], ACT.Tanh,
                                                 scale=0.5).then_inc(tanh_done, 1)
                        if kind == NEG_T:
                            copy_neg(g + 1 - n, n, bank(slot))
                        slot += 1
                    if more:
                        exps(*after, [G - 1])
                    if s % NT == NT - 1:
                        act.wait_ge(pv_done, STEPS * g + s + 1 + SLOTS)
                        nc.scalar.activation(acc_sb[:, s // NT, :], acc_ps[:, :], ACT.Copy).then_inc(acc_copied, 1)

            act.wait_ge(q_step, Q_STEPS)
            exps(0, 1, range(G))
            with act.Fori(0, NG // 2 - 1) as pair:
                group(pair * 2, 3)
                group(pair * 2 + 1, 3)
            group(NG - 2, 2)
            group(NG - 1, 1)

        @block.vector
        def _(dve):
            dve.sem_inc(normed, 1)
            dve.sem_inc(acc_copied, 1)
            for i in range(2):
                nc.vector.memset(v_grp[i][:, :, :], 0.0)
            nc.vector.memset(neg_max[:, :, :], 0.0)
            dve.drain()
            for i in range(2):
                nc.vector.memset(v_grp[i][:, :, HD:HD + 1], 1.0).then_inc(ones_done, 1)

            def moments(b, before):
                dve.wait_ge(x_in[b], 16)
                for n in range(b * NT, (b + 1) * NT):
                    nc.vector.bn_stats(stats[:, n, :], y_all[:, n, :]).then_inc(stat, 1)
                dve.wait_ge(stat, before + NT)
                for n in range(b * NT, (b + 1) * NT):
                    nc.vector.bn_aggr(mv[:, n, :], stats[:, n, :]).then_inc(stat, 1)

            def add_eps(tiles, before):
                dve.wait_ge(stat, before)
                nc.vector.tensor_scalar(ve[:, tiles], mv[:, tiles, 1], EPS, None, ALU.add).then_inc(stat, 1)

            def root(tiles, i):
                n = 5 * i
                dve.wait_ge(sd_done, i + 1)
                nc.vector.reciprocal(rc[:, tiles], sd[:, tiles]).then_inc(newton, 1)
                dve.wait_ge(newton, n + 1)
                nc.vector.tensor_tensor(nw[:, tiles], ve[:, tiles], rc[:, tiles], ALU.mult).then_inc(newton, 1)
                dve.wait_ge(newton, n + 2)
                nc.vector.tensor_tensor(nw[:, tiles], nw[:, tiles], rc[:, tiles], ALU.mult).then_inc(newton, 1)
                dve.wait_ge(newton, n + 3)
                nc.vector.tensor_scalar(nw[:, tiles], nw[:, tiles], -0.5, 1.5, ALU.mult, ALU.add).then_inc(newton, 1)
                dve.wait_ge(newton, n + 4)
                nc.vector.tensor_tensor(rstd[:, tiles], nw[:, tiles], rc[:, tiles], ALU.mult).then_inc(newton, 1)
                dve.wait_ge(newton, n + 5)
                nc.vector.scalar_tensor_tensor(shift[:, tiles], mv[:, tiles, 0], -1.0, rstd[:, tiles], ALU.mult,
                                               ALU.mult).then_inc(rstd_done, 1)

            def rotate(h, n):
                dve.wait_ge(proj_ps, 2 * h + n + 1)
                nc.vector.scalar_tensor_tensor((t1, t2)[n][:, HALF[h]], s_ps[:, n, h, :],
                                               bias_sb[:, B_S0 + n:B_S0 + n + 1], rope[:, n, HALF[h]], ALU.add,
                                               ALU.mult).then_inc(rope_mul, 1)

            moments(0, 0)
            add_eps(slice(0, NT), 2 * NT)
            root(slice(0, NT), 0)
            dve.wait_ge(rstd_done, 1)
            normalise(dve, nc.vector, 0, xn_done, halves=2)
            moments(1, 2 * NT + 1)
            add_eps(slice(NT, 2 * NT), 4 * NT + 1)
            root(slice(NT, 2 * NT), 1)
            dve.wait_ge(const_in, 48)
            for h in range(2):
                rotate(h, 0)
                rotate(h, 1)
                dve.wait_ge(rope_mul, 2 * (h + 1))
                nc.vector.tensor_tensor(rot[:, HALF[h]], t1[:, HALF[h]], t2[:, HALF[h]], ALU.add)\
                    .then_inc(rope_sum, 1)
            for h in range(2):
                dve.wait_ge(rope_sum, h + 1)
                dve.wait_ge(part_hi, h + 1)
                nc.vector.tensor_tensor(res[:, HALF[h]], rot[:, HALF[h]], part[:, 0, 0, HALF[h]],
                                        ALU.subtract).then_inc(part_res, 1)
            for h in range(2):
                dve.wait_ge(part_res, h + 1)
                dve.wait_ge(part_mid, h + 1)
                nc.vector.tensor_tensor(part[:, 0, 2, HALF[h]], res[:, HALF[h]], part[:, 0, 1, HALF[h]],
                                        ALU.subtract).then_inc(part_lo, 1)
            for b in range(2, B):
                moments(b, 2 * b * NT + 2)
            add_eps(slice(2 * NT, NTT), 2 * NTT + 2)
            root(slice(2 * NT, NTT), 2)
            nc.vector.tensor_copy(ident16[:, :], ident[:, :]).then_inc(id_done, 1)
            dve.wait_ge(ffn_in, 16)
            nc.vector.tensor_scalar(w_ffn[:, :], wi_sb[:, :], DEQUANT, None, ALU.mult).then_inc(w_done, 1)

            def reduce_max(g, a, ps):
                dve.wait_ge(a_ready, AU * g + a + 1)
                h, a = a % AU // HU, a % HU
                nc.vector.tensor_reduce(out=mx[:, h, a // 2, a % 2:a % 2 + 1], in_=ps, op=ALU.max,
                                        axis=AX.X).then_inc(max_done, 1)

            def split_neg(g, h, step):
                n = NEG * (NH * g + h)
                if step == 0:
                    dve.wait_ge(max_done, HU * (NH * g + h + 1))
                    made = nc.vector.tensor_tensor(row_max[:, :], mx[:, h, :, 0], mx[:, h, :, 1], ALU.max)
                else:
                    dve.wait_ge(neg_step, n + step)
                if step == 1:
                    made = nc.vector.tensor_scalar(neg_max[:, 0, :], row_max[:, :], -1.0, None, ALU.mult)
                elif step == 2:
                    made = nc.vector.scalar_tensor_tensor(rest[:, :], row_max[:, :], -1.0, neg_max[:, 0, :], ALU.mult,
                                                          ALU.subtract)
                elif step == 3:
                    made = nc.vector.tensor_copy(neg_max[:, 1, :], rest[:, :])
                elif step == 4:
                    made = nc.vector.tensor_tensor(neg_max[:, 2, :], rest[:, :], neg_max[:, 1, :], ALU.subtract)
                made.then_inc(neg_step, 1)

            def maximum(g, a, ps, last_unit=False):
                reduce_max(g, a, ps)
                done, step = divmod(a + 1, HU)
                if done and step < NEG:
                    half = done - 1
                    for i in range(step, NEG if last_unit else step + 1):
                        split_neg(g + half // NH, half % NH, i)

            for a in range(LEAD):
                maximum(0, a, first_bank(first_slot(a)))

            def hidden(g, c, ps):
                dve.wait_ge(tanh_done, FC * g + c + 1)
                nc.vector.scalar_tensor_tensor(gated[:, c, :], th[:, c, :], 1.0, ps[:, 0:CH], ALU.add,
                                               ALU.mult).then_inc(gated_done, 1)
                dve.wait_ge(gated_done, FC * g + c + 1)
                nc.vector.scalar_tensor_tensor(hid[:, c, :], gated[:, c, :], 0.5, ps[:, CH:2 * CH],
                                               ALU.mult, ALU.mult).then_inc(hid_done, 1)

            def add_ffn(g, ps):
                dve.wait_ge(bo_added, B)
                dve.wait_ge(ffn_down, g + 1)
                chunk = y_all[:, bass.ds(g * CT, CT), :]
                nc.vector.tensor_tensor(chunk, chunk, ps[:, 0:CT * D].rearrange("p (t d) -> p t d", t=CT),
                                        ALU.add).then_inc(y_done, 1)

            def normalise_context(g, h, ps):
                ps = ps.rearrange("p (t j c) -> p t j c", t=HT, j=G)
                dve.wait_ge(ctx_ps, NH * g + h + 1)
                nc.vector.reciprocal(rec[:, h, :, :], ps[:, :, :, HD]).then_inc(rec_done, 1)
                dve.wait_ge(rec_done, NH * g + h + 1)
                nc.vector.tensor_tensor(context_half(g, h), ps[:, :, :, 0:HD],
                                        rec[:, h, :, :].unsqueeze(3).to_broadcast([P, HT, G, HD]),
                                        ALU.mult).then_inc(normed, 1)

            def copy_ctx_T(u, ps):
                dve.wait_ge(ctx_T_ps, u + 1)
                nc.vector.tensor_copy(ctx_T[:, (u % 2) * W:(u % 2 + 1) * W], ps).then_inc(ctx_T_done, 1)

            def add_attention(u, ps):
                dve.wait_ge(o_ps, u + 1)
                piece = y_all[:, u * HT:(u + 1) * HT, :]
                nc.vector.tensor_tensor(piece, piece, ps.rearrange("p (t d) -> p t d", d=D),
                                        ALU.add).then_inc(o_done, 1)

            def job(g, slot, kind, n):
                ps = bank(slot)
                if kind == UP:
                    hidden(g, n, ps)
                elif kind == DOWN:
                    add_ffn(g, ps)
                elif kind == CTX:
                    normalise_context(g, n, ps)
                elif kind == STAGE:
                    copy_ctx_T(n, ps)
                elif kind == PROJ:
                    add_attention(n, ps)

            def group(g, order):
                for slot, (kind, n) in enumerate(order):
                    if kind == MAX:
                        maximum(g, n, bank(slot), last_unit=order is LAST_ORDER and n == AU - 1)
                    else:
                        job(g, slot, kind, n)

            for i in range(PER):
                maximum(0, LEAD + i, bank(i - PER))
            with dve.Fori(0, NG // 2 - 1) as pair:
                group(pair * 2, ORDER)
                group(pair * 2 + 1, ORDER)
            group(NG - 2, ORDER)
            group(NG - 1, LAST_ORDER)

        @block.tensor
        def _(pe):
            pe.sem_inc(pv_done, SLOTS)
            pe.wait_ge(w_in, 32)

            def transpose_xn(b, h):
                if b == 0:
                    pe.wait_ge(xn_done, h + 1)
                elif b == B - 1:
                    pe.wait_ge(xn_done_act, 1)
                else:
                    pe.wait_ge(xn_done_pool, b)
                if b == 1 and h == 0:
                    pe.wait_ge(rope_mul, 1)
                if b >= 1:
                    pe.wait_ge(xnt_done, 2 * b + h - 1)
                if b == 2 and h == 0:
                    pe.wait_ge(raw_done, 1)
                for t in range(HT):
                    last = nc.tensor.transpose(xnt_banks[h][:, t * P:(t + 1) * P], xn[:, b, h * HT + t, :],
                                               ident[:, :])
                last.then_inc(xnt_ps, 1)

            def project(c, b, n, h):
                return nc.tensor.matmul(s_ps[:, n, h, :], wf_sb[:, c + n * D:c + (n + 1) * D],
                                        xn_T[:, b * T + h * W:b * T + (h + 1) * W], start=True, stop=True)

            def project_tiles(n, h, columns):
                for b, c in enumerate(columns):
                    last = nc.tensor.matmul(s_ps[32 * b:32 * b + 32, n, h, :], wf_sb[:, c:c + 32],
                                            xn_T[:, b * T + h * W:b * T + (h + 1) * W], start=True, stop=True)
                return last

            for h in range(2):
                transpose_xn(0, h)
            for h in range(2):
                pe.wait_ge(xnt_done, h + 1)
                for n in range(2):
                    project(C_S0, 0, n, h).then_inc(proj_ps, 1)
            for h in range(2):
                transpose_xn(1, h)
            pe.wait_ge(xnt_done, 4)
            for n in range(2):
                pe.wait_ge(rope_mul, 3 + n)
                for h in range(2):
                    last = project(C_Q, 1, n, h)
                last.then_inc(q_ps, 1)

            def max_unit(par, a, ps):
                h, r = a // HU, a % HU
                j, t, k = r // (HT * 2), h * HT + r // 2 % HT, r % 2
                nc.tensor.matmul(ps, qa[par][0:MAX_ROW, j, t * P:(t + 1) * P],
                                 ka[par][0:MAX_ROW, k * W:(k + 1) * W], start=True, stop=True).then_inc(a_ready, 1)

            def transpose_neg(g, h, ps):
                pe.wait_ge(neg_step, NEG * (NH * g + h + 1))
                nc.tensor.transpose(ps.bitcast(BF16)[0:2 * PARTS * G * HT, 0:P], neg_max[:, :, :], ident16[:, :])\
                    .then_inc(neg_T_ps, 1)

            def scores(g, par, s, j):
                kt, h = s % NT, s // NT
                u = G * s + j
                if kt == 0 and j == 0:
                    pe.wait_ge(neg_loaded, (NH * g + h + 1) * 16)
                pe.wait_ge(exp_done, SG * g + score_before(u) + 1 + G)
                nc.tensor.matmul(banks[:, score_bank(u), :], kc[par][:, kt * P:(kt + 1) * P],
                                 qc[par][:, h, j, :], start=True, stop=True).then_inc(scores_ready, 1)

            pe.wait_ge(qa_loaded[0], DMAS)
            for a in range(LEAD):
                if a >= FIRST_RING:
                    pe.wait_ge(max_done, a + 1 - FIRST_RING + (NEG_BEHIND < a <= NEG_BEHIND + FIRST_RING))
                if a == NEG_BEHIND + FIRST_RING:
                    pe.wait_ge(neg_T_done, 1)
                max_unit(0, a, first_bank(first_slot(a)))
                if a in PE_XN:
                    transpose_xn(2 + PE_XN.index(a) // 2, PE_XN.index(a) % 2)
                if a in PE_S1:
                    n, h = divmod(PE_S1.index(a), 2)
                    if h == 0:
                        pe.wait_ge(xnt_done, 2 * B)
                        pe.wait_ge(raw_done, n + 1)
                    last = project_tiles(n, h, [C_Q + n * D + Q_ROWS] + [C_K + n * 32] * (B - 1))
                    if h == 1:
                        last.then_inc(q_ps, 1)
                if a in PE_V:
                    h = PE_V.index(a)
                    if h == 0:
                        pe.wait_ge(raw_done, 3)
                    last = project_tiles(0, h, [C_V] * B)
                    if h == 1:
                        last.then_inc(vt_ps, 1)
                if a in PE_VT:
                    h = PE_VT.index(a)
                    if h == 0:
                        pe.wait_ge(vt_done, 1)
                        pe.wait_ge(raw_done, 4)
                    for t in range(h * HT, (h + 1) * HT):
                        last = nc.tensor.transpose(s_ps[:, 1, t // 4, t % 4 * P:(t % 4 + 1) * P],
                                                   v_T[:, t * P:(t + 1) * P], ident[:, :])
                    if h == 1:
                        last.then_inc(v_ps, 1)
                if a in PE_Q:
                    b, n, h = 2 + PE_Q.index(a) // 4, PE_Q.index(a) // 2 % 2, PE_Q.index(a) % 2
                    if h == 0:
                        if b > 2:
                            pe.wait_ge(raw_done, 2 * (b - 1) + n + 1)
                        elif n == 1:
                            pe.wait_ge(v_done, 1)
                    last = project(C_Q, b, n, h)
                    if h == 1:
                        last.then_inc(q_ps, 1)
                if a == NEG_BEHIND:
                    pe.wait_ge(id_done, 1)
                    pe.wait_ge(max_done, a - 1)
                    transpose_neg(0, 0, first_bank(NEG_BEHIND + 1))
            pe.wait_ge(raw_done, 2 * B)
            pe.wait_ge(w_done, 1)
            pe.wait_ge(qc_loaded[0], DMAS_C)
            for j in range(G):
                scores(0, 0, 0, j)

            def weigh(g, par, s):
                kt, h = s % NT, s // NT
                if s == 0:
                    pe.wait_ge(v_grp_done, g + 1)
                if kt == 0:
                    pe.wait_ge(acc_copied, NH * g + h + 1)
                pe.wait_ge(exp_done, SG * g + G * (s + 1) + G)
                for j in range(G):
                    last = nc.tensor.matmul(acc_ps[VC * j:VC * (j + 1), :], v_grp[par][:, kt, :],
                                            probs[:, s % SLOTS, j, :], start=(kt == 0), stop=(kt == NT - 1))
                last.then_inc(pv_done, 1)

            def ffn_gate_up(g, c, ps):
                for n in range(2):
                    last = nc.tensor.matmul(ps[:, n * CH:(n + 1) * CH],
                                            w_ffn[:, n * HID + c * P:n * HID + (c + 1) * P],
                                            xn_T[:, bass.ds(g * CH, CH)], start=True, stop=True)
                last.then_inc(ffn_up, 1)

            def ffn_down_proj(g, ps):
                pe.wait_ge(hid_done, FC * (g + 1))
                for t in range(CT):
                    for c in range(FC):
                        last = nc.tensor.matmul(ps[:, t * D:(t + 1) * D], hid[:, c, t * P:(t + 1) * P],
                                                w_ffn[:, 2 * HID + c * D:2 * HID + (c + 1) * D],
                                                start=(c == 0), stop=(c == FC - 1))
                last.then_inc(ffn_down, 1)

            def transpose_context(g, h, ps):
                pe.wait_ge(acc_copied, NH * g + h + 2)
                for t in range(HT):
                    last = nc.tensor.transpose(ps[:, t * P:(t + 1) * P], acc_sb[:, h, t * P:(t + 1) * P],
                                               ident[:, :])
                last.then_inc(ctx_ps, 1)

            def transpose_stage(u, ps):
                b, h = u // 2, u % 2
                pe.wait_ge(normed, NH * (KV * b + KV - 1) + h + 2)
                for t in range(HT):
                    last = nc.tensor.transpose(ps[:, t * P:(t + 1) * P],
                                               ctx_all[:, h * HT + t, b * KV:(b + 1) * KV, :]
                                               .rearrange("p g c -> p (g c)"), ident[:, :])
                last.then_inc(ctx_T_ps, 1)

            def project_out(u, ps):
                pe.wait_ge(ctx_T_done, u + 1)
                for t in range(HT):
                    c = (u % 2) * W + t * P
                    last = nc.tensor.matmul(ps[:, t * D:(t + 1) * D], ctx_T[:, c:c + P], wf_sb[:, C_O:C_O + D],
                                            start=True, stop=True)
                last.then_inc(o_ps, 1)

            def bank_left(g, kind, n, back=0):
                if kind == MAX:
                    pe.wait_ge(max_done, AU * g + n + 1 - AU * back)
                elif kind == UP:
                    pe.wait_ge(hid_done, FC * g + n + 1 - FC * back)
                elif kind == DOWN:
                    pe.wait_ge(y_done, g + 1 - back)
                elif kind == NEG_T:
                    pe.wait_ge(neg_T_done, NH * g + NH * (1 - n) + n + 1 - NH * back)
                elif kind == CTX:
                    pe.wait_ge(normed, NH * g + n + 2 - NH * back)
                elif kind == STAGE:
                    pe.wait_ge(ctx_T_done, n + 1)
                elif kind == PROJ:
                    pe.wait_ge(o_done, n + 1)

            def take(g, par, slot, order):
                if slot >= RING:
                    bank_left(g, *order[slot - RING])
                else:
                    bank_left(g, *ORDER[slot - RING], back=1)
                kind, n = order[slot]
                ps = bank(slot)
                if kind == MAX:
                    max_unit(par if n < AU else 1 - par, n % AU, ps)
                elif kind == UP:
                    ffn_gate_up(g, n, ps)
                elif kind == DOWN:
                    ffn_down_proj(g, ps)
                elif kind == NEG_T:
                    transpose_neg(g + 1 - n, n, ps)
                elif kind == CTX:
                    transpose_context(g, n, ps)
                elif kind == STAGE:
                    transpose_stage(n, ps)
                elif kind == PROJ:
                    project_out(n, ps)

            def next_scores(g, pair, par, s, j):
                s += 1
                if s == STEPS and j == 0:
                    if par == 0:
                        pe.wait_ge(qc_loaded[1], (pair + 1) * DMAS_C)
                    else:
                        pe.wait_ge(qc_loaded[0], (pair + 2) * DMAS_C)
                scores(g + s // STEPS, par if s < STEPS else 1 - par, s % STEPS, j)

            def group(g, pair, par, left):
                order = LAST_ORDER if left == 1 else ORDER
                slot = 0
                for s in range(1, STEPS + (left > 1)):
                    if PER * s + LEAD == AU and left > 1:
                        if par == 0:
                            pe.wait_ge(qa_loaded[1], (pair + 1) * DMAS)
                        else:
                            pe.wait_ge(qa_loaded[0], (pair + 2) * DMAS)
                    if PER * (s + 1) + LEAD == AU and left > 2:
                        pe.wait_ge(q_stored, pair + 1)
                    todo = step_order(s, left == 1)
                    units = [o for o in todo if o[0] == MAX]
                    more = s + 1 < STEPS or left > 1
                    jobs_at = G - 1 if units else G - 2
                    for j in range(G):
                        if j == jobs_at:
                            for _ in range(len(todo) - len(units)):
                                take(g, par, slot, order)
                                slot += 1
                        if j == G - 1:
                            weigh(g + s // STEPS, par if s < STEPS else 1 - par, s % STEPS)
                        if units:
                            take(g, par, slot, order)
                            slot += 1
                        if more:
                            next_scores(g, pair, par, s, j)
                for slot in range(slot, len(order)):
                    take(g, par, slot, order)

            for i in range(PER):
                if i > 0:
                    pe.wait_ge(max_done, LEAD + i - FIRST_RING)
                if i == PER - 1:
                    weigh(0, 0, 0)
                max_unit(0, LEAD + i, bank(i - PER))
                scores(0, 0, 1, i)

            with pe.Fori(0, NG // 2 - 1) as pair:
                group(pair * 2, pair, 0, 3)
                group(pair * 2 + 1, pair, 1, 3)
            group(NG - 2, NG // 2 - 1, 0, 2)
            group(NG - 1, NG // 2 - 1, 1, 1)


_INS = ["x", "wf", "wi", "biases", "bo", "tables", "identity"]


def kernel(**inputs):
    import numpy as np
    import concourse.bacc as bacc
    from concourse.bass_utils import run_bass_kernel_spmd

    p = "L0_attn_"
    a = {k: np.asarray(v) for k, v in inputs.items()}
    half = [1, 3, 5, 7, 0, 2, 4, 6]
    q_rows = [h * HD + r for h in range(H) for r in half]
    k_rows = [h * HD + r for h in range(KV) for r in half]
    wq, wk, wv, wo = (a[p + n] for n in ("Wq", "Wk", "Wv", "Wo"))
    bq, bk, bv = (a[p + n] for n in ("bq", "bk", "bv"))
    first, first_rotated = (np.concatenate([q[:Q_ROWS], k]) for q, k in ((wq, wk), (wq[q_rows], wk[k_rows])))
    wf = np.concatenate([first.T, first_rotated.T, wq.T, wq[q_rows].T, wk.T, wk[k_rows].T, wv.T, wo.T], axis=1)
    down = a["L0_ffn_w_down"].T.reshape(FC, P, D).transpose(1, 0, 2).reshape(P, FC * D)
    wi = np.concatenate([a["L0_ffn_w_gate"].T, a["L0_ffn_w_up"].T, down], axis=1)
    b_q = [bq, bq[q_rows]]
    b_k = [bk, bk[k_rows]]
    biases = np.stack([np.concatenate([q[:Q_ROWS], k]) for q, k in zip(b_q, b_k)]
                      + [np.concatenate([q[Q_ROWS:]] + [k] * (B - 1)) for q, k in zip(b_q, b_k)]
                      + b_q + [np.tile(bv, B)], axis=1)
    freq = (np.float32(1.0) / np.float32(10000.0) ** (np.arange(0, HD, 2, dtype=np.float32) / np.float32(HD)))
    angle = np.arange(T, dtype=np.float32)[None, :] * freq.astype(np.float32)[:, None]
    cos = np.tile(np.cos(angle), (P // len(freq), 1))
    sin = np.tile(np.concatenate([-np.sin(angle), np.sin(angle)], axis=0), (P // HD, 1))
    tables = np.stack([cos, sin], axis=1).astype(np.float32)

    arrays = {
        "x": a[p + "hidden_states"], "wf": wf, "wi": wi, "biases": biases, "bo": a[p + "bo"], "tables": tables,
        "identity": np.eye(P, dtype=np.float32),
    }
    nc = bacc.Bacc("TRN2", target_bir_lowering=False, num_devices=1)
    arrays = {f"in_{n}": np.ascontiguousarray(arrays[n]) for n in _INS}
    aps = [nc.dram_tensor(n, v.shape, mybir.dt.from_np(v.dtype), kind="ExternalInput").ap() for n, v in arrays.items()]
    out = nc.dram_tensor("out_0", (B, T, D), F32, kind="ExternalOutput").ap()
    attention_swiglu(nc, *aps, out)
    r = run_bass_kernel_spmd(nc, [arrays], core_ids=[0])
    return r.results[0]["out_0"]
```
